# Optimizing a Trainium2 kernel written in Bass

```python
import numpy as np
import jax
import jax.numpy as jnp

def _softmax(x, axis=-1):
    return jax.nn.softmax(x, axis=axis)
def _gelu(x):
    return jax.nn.gelu(x, approximate=True)
def _silu(x):
    return jax.nn.silu(x)
def _sigmoid(x):
    return jax.nn.sigmoid(x)
def _layernorm(x, axis=-1, eps=1e-5):
    m = jnp.mean(x, axis=axis, keepdims=True)
    v = jnp.var(x, axis=axis, keepdims=True)
    return (x - m) / jnp.sqrt(v + eps)
def _scatter_add(tgt, idx, src, axis=0):
    return tgt.at[idx].add(src)
def _segment_sum(src, seg, n):
    return jax.ops.segment_sum(src, seg, n)

kernel_name = 'mk_adj_preln_d1_adj_512_4799a3'

def setup_inputs(seed: int = 0):
    np.random.seed(seed)
    _w = jnp.asarray
    def _rec_inputs():
        import jax
        import jax.numpy as jnp
        _gk = jax.random.key(seed)
        x = -0.0002928 + 1 * jax.random.normal(jax.random.fold_in(_gk, 1), (8192, 512), jnp.float32)
        _a = jax.random.bernoulli(jax.random.fold_in(_gk, 2), 0.000488281, (8192, 8192))
        _a = jnp.logical_or(_a, jnp.swapaxes(_a, -1, -2))
        _a = jnp.logical_or(_a, jnp.eye(8192, dtype=bool))
        _af = _a.astype(jnp.float32)
        _af = _af * jax.random.uniform(jax.random.fold_in(_gk, 3), (8192, 8192), jnp.float32, 0.05, 5.41998)
        adj = _af
        return x, adj
    x, adj = _rec_inputs()
    def _L0_gnn_setup():
        import jax, jax.numpy as jnp
        import numpy as np
        N = 8192
        D = 512
        EPS = 1e-12
        key = jax.random.key(seed)
        k1, k2 = jax.random.split(key)
        cur = jax.random.normal(k1, (N, D), dtype=jnp.float32)
        incidence_m = jax.random.normal(k2, (N, N), dtype=jnp.float32)
        return {'cur': cur, 'incidence_m': incidence_m}
    _L0_gnn_all = _L0_gnn_setup()
    _L0_gnn_in = {k: v for k, v in _L0_gnn_all.items() if k in ()}
    del _L0_gnn_all

    return {
        "x": x,
        "adj": adj,
    }

def reference(x, adj):
    import jax
    import jax.numpy as jnp
    def _L0_gnn_ref(cur, incidence_m):
        import jax, jax.numpy as jnp
        import numpy as np
        N = 8192
        D = 512
        EPS = 1e-12
        mask = incidence_m > 0
        head = jax.lax.stop_gradient(mask.astype(incidence_m.dtype))
        head = head / jnp.maximum(jnp.sqrt(jnp.sum(head * head, axis=-1, keepdims=True)), EPS)
        inc = incidence_m + head
        edge_fea = inc @ cur
        edge_degree = jnp.sum(inc, axis=-1, keepdims=True)
        return edge_fea / edge_degree

    h = jnp.maximum(_layernorm(x, axis=-1), 0.0)
    x = x + _L0_gnn_ref(h, adj)
    return x


_drawn_inputs = setup_inputs


def setup_inputs(seed=0):
    import zlib

    import numpy as np

    out = dict(_drawn_inputs(seed))
    spreads = {}
    factors = {}
    for name, (base, spread) in spreads.items():
        noise = np.random.default_rng([zlib.crc32(name.encode()), seed]).standard_normal(out[name].shape)
        drawn = base * np.exp(spread * noise) if base else spread * noise
        out[name] = jnp.asarray(drawn.astype(out[name].dtype))
    for name, factor in factors.items():
        out[name] = (out[name] * factor).astype(out[name].dtype)
    return out
```

```python
import concourse.bass as bass
from concourse import mybir
from contextlib import ExitStack

P = 128


def add_graph_layer(nc, x, adj, out):
    fp32 = mybir.dt.float32
    bf16 = mybir.dt.bfloat16
    u32 = mybir.dt.uint32
    ALU = mybir.AluOpType
    ACT = mybir.ActivationFunctionType
    AX = mybir.AxisListType

    N, D = x.shape
    TILES = N // P
    EPS_NORM = 1e-5
    EPS_HEAD = 1e-12

    SEGS = 8
    SEG = N // SEGS
    CAND = 8 * SEGS
    QUARTERS = 4
    QCOLS = N // QUARTERS
    SEGS_Q = SEGS // QUARTERS
    SLOTS = 24
    BIAS = 128
    TOP = BIAS + N - 1
    FIXED = 16
    EXTRA = [(16, 18), (18, 20), (20, 24)]
    DIAG_GROUPS = [(0, 8), (8, 16), (16, 24)]

    ROWS = 4
    LN = N // (P * ROWS)
    KB = N // P
    HCH = 8
    NCH = KB // HCH

    x_ln = x.rearrange("(c p j) d -> c p j d", p=P, j=ROWS)
    x_t = x.rearrange("(t p) d -> t p d", p=P)
    out_t = out.rearrange("(t p) d -> t p d", p=P)
    adj_t = adj.rearrange("(t p) n -> t p n", p=P)

    ctx = ExitStack()
    with ctx:
        def sb(name, shape, dt):
            return ctx.enter_context(nc.sbuf_tensor(name, shape, dt))

        def sem(name):
            return ctx.enter_context(nc.semaphore(name))

        h = nc.dram_tensor("h_scratch", [N, D], fp32, kind="Internal").ap()
        h_ln = h.rearrange("(c p j) d -> c p j d", p=P, j=ROWS)
        h_blk = h.rearrange("(c k p) d -> c p k d", p=P, k=HCH)

        A = sb("adj_tile", [P, 2, N], fp32)
        G = sb("gathered", [P, 2, SLOTS, D], fp32)
        diag = sb("diag", [P, 2, SLOTS, P], fp32)
        ident = sb("ident", [P, P], fp32)
        ones = sb("ones", [P, 1], fp32)
        junk = sb("junk", [P, 2, QCOLS], bf16)
        xres = sb("x_residual", [P, 2, D], fp32)
        osb = sb("out_tile", [P, 2, D], fp32)
        cv = sb("cand_value", [P, CAND], fp32)
        ci = sb("cand_index", [P, CAND], u32)
        cpos = sb("cand_positive", [P, CAND], fp32)
        segtab = sb("segment_key", [P, SEGS], fp32)
        key0 = sb("key0", [P, CAND], u32)
        key = sb("key", [P, CAND], u32)
        khi = sb("key_high", [P, CAND], u32)
        klo = sb("key_low", [P, CAND], u32)
        shi = sb("sorted_high", [P, SLOTS], u32)
        slo = sb("sorted_low", [P, SLOTS], u32)
        su = sb("slot_rank", [P, SLOTS], u32)
        sl16 = sb("slot_low16", [P, SLOTS], u32)
        idx = sb("slot_column", [P, 2, SLOTS], u32)
        val = sb("slot_value", [P, 2, SLOTS], u32)
        pos = sb("slot_positive", [P, SLOTS], fp32)
        inc = sb("slot_inc", [P, 2, SLOTS], fp32)
        cnt = sb("count", [P, 2], fp32)
        full = sb("full_segments", [P, 1], fp32)
        fullf = sb("full_flags", [P, SEGS], fp32)
        neg = sb("negatives", [P, 2, QUARTERS], fp32)
        negf = sb("negative_flags", [P, QUARTERS], fp32)
        negs = sb("negative_count", [P, 1], fp32)
        over = sb("overfull", [P, 1], fp32)
        limits = sb("limits", [P, len(EXTRA)], fp32)
        flags = sb("flags", [P, len(EXTRA) + 1], fp32)
        need = sb("need", [1, 2, 2 * len(EXTRA)], u32)
        used = sb("used", [1, 2, len(EXTRA)], fp32)
        root = sb("root", [P, 2], fp32)
        rootc = sb("root_clamped", [P, 1], fp32)
        head = sb("head", [P, 1], fp32)
        deg = sb("degree", [P, 1], fp32)
        rdeg = sb("inv_degree", [P, 2], fp32)
        tnum = sb("tile_number", [1, TILES], fp32)
        bad = sb("bad", [1, TILES], fp32)
        badk = sb("bad_key", [1, TILES], fp32)
        badl = sb("bad_list", [1, TILES], fp32)
        badu = sb("bad_list_int", [1, TILES], u32)
        badn = sb("bad_number", [1, 1], fp32)
        badnu = sb("bad_number_int", [1, 1], u32)
        xin = A[:, 0, :].rearrange("p (b j d) -> p b j d", b=4, j=ROWS)
        hst = A[:, 1, :].rearrange("p (b j d) -> p b j d", b=4, j=ROWS)
        st = sb("ln_stats", [P, 2, ROWS, 6], fp32)
        mv = sb("ln_mean_var", [P, 2, ROWS, 2], fp32)
        ve = sb("ln_var_eps", [P, 2, ROWS], fp32)
        sd = sb("ln_std", [P, 2, ROWS], fp32)
        rs = sb("ln_rstd", [P, 2, ROWS], fp32)
        nb = sb("ln_bias", [P, 2, ROWS], fp32)
        incT = sb("inc_T", [P, 2, P], fp32)
        dcnt = sb("dense_count", [P, 1], fp32)
        drt = sb("dense_root", [P, 1], fp32)
        drc = sb("dense_root_clamped", [P, 1], fp32)
        dhd = sb("dense_head", [P, 1], fp32)
        ddeg = sb("dense_degree", [P, 1], fp32)
        drd = sb("dense_inv_degree", [P, 1], fp32)

        acc = [ctx.enter_context(nc.psum_tensor(f"acc{b}", [P, D], fp32)) for b in range(2)]
        pflag = ctx.enter_context(nc.psum_tensor("pflag", [P, 512], fp32))
        ptr = [ctx.enter_context(nc.psum_tensor(f"ptr{b}", [P, 512], fp32)) for b in range(2)]
        pdense = ctx.enter_context(nc.psum_tensor("pdense", [P, D], fp32))

        const_step = sem("const_step")
        passed = sem("passed")
        consts_set = sem("consts_set")
        zeroed = sem("zeroed")
        ln_loaded = [sem(f"ln_loaded{b}") for b in range(4)]
        ln_stat = sem("ln_stat")
        ln_var = sem("ln_var")
        ln_root = sem("ln_root")
        ln_scaled = sem("ln_scaled")
        ln_done = sem("ln_done")
        h_stored = [sem(f"h_stored{b}") for b in range(4)]
        adj_loaded = [[sem(f"adj_loaded{b}{q}") for q in range(QUARTERS)] for b in range(2)]
        x_loaded = [sem(f"x_loaded{b}") for b in range(2)]
        negs_checked = sem("negs_checked")
        vals_found = sem("vals_found")
        idx_found = sem("idx_found")
        pack = sem("pack")
        cols_ready = sem("cols_ready")
        count_ready = sem("count_ready")
        flags_ready = sem("flags_ready")
        flags_summed = sem("flags_summed")
        used_counted = sem("used_counted")
        need_ready = sem("need_ready")
        root_ready = sem("root_ready")
        weigh = sem("weigh")
        inc_ready = sem("inc_ready")
        diag_ready = sem("diag_ready")
        gathered = [[sem(f"gathered{b}{g}") for g in range(2 + len(EXTRA))] for b in range(2)]
        acc_ready = sem("acc_ready")
        out_ready = sem("out_ready")
        out_stored = [sem(f"out_stored{b}") for b in range(2)]
        list_step = sem("list_step")
        list_ready = sem("list_ready")
        d_adj = sem("d_adj")
        d_x = sem("d_x")
        d_h = [sem(f"d_h{b}") for b in range(2)]
        d_step = sem("d_step")
        d_count = sem("d_count")
        d_root = sem("d_root")
        d_inc = sem("d_inc")
        d_tr = sem("d_tr")
        d_copied = sem("d_copied")
        d_mm = sem("d_mm")
        d_out = sem("d_out")
        d_stored = sem("d_stored")

        def hold(eng, signal, value):
            eng.wait_ge(signal, value)
            eng.sem_inc(passed, 1)

        block = ctx.enter_context(nc.Block())
        LAST = TILES // 2 - 1

        @block.sync
        def _(sp):
            def ln_load(i, b):
                sp.dma_start(xin[:, b], x_ln[i * 4 + b]).then_inc(ln_loaded[b], 16)

            def ln_store(i, b):
                sp.wait_ge(ln_done, i * 4 + b + 1)
                sp.dma_start(h_ln[i * 4 + b], hst[:, b]).then_inc(h_stored[b], 16)

            for b in range(4):
                ln_load(0, b)
            with sp.Fori(1, LN // 4) as i:
                for b in range(4):
                    ln_store(i - 1, b)
                    ln_load(i, b)
            for b in range(4):
                ln_store(LN // 4 - 1, b)

            def load_tile(i, b, first=False):
                for q in range(QUARTERS):
                    if not first:
                        hold(sp, idx_found, i * (2 * SEGS) + (b - 2) * SEGS + (q + 1) * SEGS_Q)
                        sp.wait_ge(negs_checked, i * (2 * QUARTERS) + (b - 2) * QUARTERS + q + 1)
                    sp.dma_start(A[:, b, q * QCOLS:(q + 1) * QCOLS],
                                 adj_t[i * 2 + b, :, q * QCOLS:(q + 1) * QCOLS]).then_inc(adj_loaded[b][q], 16)
                if not first:
                    store_tile(i - 1, b)
                    sp.wait_ge(out_stored[b], i * 16)
                sp.dma_start(xres[:, b], x_t[i * 2 + b]).then_inc(x_loaded[b], 16)

            def store_tile(i, b):
                hold(sp, out_ready, i * 2 + b + 1)
                sp.dma_start(out_t[i * 2 + b], osb[:, b]).then_inc(out_stored[b], 16)

            for b in range(4):
                sp.wait_ge(h_stored[b], 16 * (LN // 4))
            for b in range(2):
                load_tile(0, b, first=True)
            with sp.Fori(1, TILES // 2) as i:
                for b in range(2):
                    load_tile(i, b)
            for b in range(2):
                store_tile(LAST, b)
            for b in range(2):
                sp.wait_ge(out_stored[b], 16 * (TILES // 2))

            sp.wait_ge(list_ready, 1)
            n = sp.value_load(badnu[0:1, 0:1], min_val=0, max_val=TILES)
            with sp.If(n > 0):
                with sp.Fori(0, n) as j:
                    t = sp.value_load(badu[0:1, bass.ds(j, 1)], min_val=0, max_val=TILES - 1)
                    sp.dma_start(A[:, 0, :], adj_t[t]).then_inc(d_adj, 16)
                    sp.dma_start(xres[:, 0], x_t[t]).then_inc(d_x, 16)
                    for c in range(NCH):
                        if c >= 2:
                            sp.wait_ge(d_mm, j * KB + (c - 1) * HCH)
                        sp.dma_start(G[:, c % 2, 0:HCH, :], h_blk[c]).then_inc(d_h[c % 2], 16)
                    sp.wait_ge(d_out, j + 1)
                    sp.dma_start(out_t[t], osb[:, 0]).then_inc(d_stored, 16)
                    hold(sp, d_stored, j * 16 + 16)

        @block.gpsimd
        def _(pool):
            steps = [0]

            def step(ins):
                steps[0] += 1
                ins.then_inc(const_step, 1)
                pool.wait_ge(const_step, steps[0])

            step(nc.gpsimd.memset(ident[:], 0.0))
            step(nc.gpsimd.affine_select(out=ident[:], in_=ident[:], compare_op=ALU.not_equal, fill=1.0,
                                         base=0, pattern=[[-1, P]], channel_multiplier=1))
            step(nc.gpsimd.memset(ones[:], 1.0))
            step(nc.gpsimd.memset(used[:], 0.0))
            step(nc.gpsimd.iota(tnum[:], pattern=[[1, TILES]], base=1, channel_multiplier=0,
                                allow_small_or_imprecise_dtypes=True))
            for s in range(SEGS):
                step(nc.gpsimd.memset(segtab[:, s:s + 1], float((TOP - SEG * s) * 65536)))
            for k, (lo, _) in enumerate(EXTRA):
                step(nc.gpsimd.memset(limits[:, k:k + 1], float(lo)))
            pool.sem_inc(consts_set, 1)
            nc.gpsimd.memset(G[:, 0], 0.0).then_inc(zeroed, 1)
            nc.gpsimd.memset(G[:, 1], 0.0).then_inc(zeroed, 1)

            pool.wait_ge(zeroed, 2)
            for b in range(4):
                pool.wait_ge(h_stored[b], 16 * (LN // 4))

            def gather(b, s, done):
                nc.gpsimd.indirect_dma_start(
                    out=G[:, b, s, :], out_offset=None, in_=h[:, :],
                    in_offset=bass.IndirectOffsetOnAxis(ap=idx[:, b, s:s + 1], axis=0),
                    bounds_check=N - 1, oob_is_err=False).then_inc(done, 16)

            def gather_tile(i, b, first=False):
                if not first:
                    pool.wait_ge(acc_ready, i * 2 + b - 1)
                hold(pool, cols_ready, i * 2 + b + 1)
                for s in range(FIXED):
                    gather(b, s, gathered[b][s // 8])
                hold(pool, need_ready, i * 4 + b * 2 + 2)
                for k, (lo, hi) in enumerate(EXTRA):
                    v = pool.value_load(need[0:1, b, k:k + 1], min_val=0, max_val=P)
                    with pool.If(v > 0):
                        for s in range(lo, hi):
                            gather(b, s, gathered[b][2 + k])

            for b in range(2):
                gather_tile(0, b, first=True)
            with pool.Fori(1, TILES // 2) as i:
                for b in range(2):
                    gather_tile(i, b)

        @block.scalar
        def _(act):
            def ln_sqrt(i, b):
                act.wait_ge(ln_var, i * 4 + b + 1)
                nc.scalar.activation(sd[:, b % 2], ve[:, b % 2], ACT.Sqrt).then_inc(ln_root, 1)

            def ln_apply(i, b, first=False):
                act.wait_ge(ln_scaled, i * 4 + b + 1)
                if not first:
                    act.wait_ge(h_stored[b], i * 16)
                for j in range(ROWS):
                    last = nc.scalar.activation(hst[:, b, j], xin[:, b, j], ACT.Relu,
                                                bias=nb[:, b % 2, j:j + 1], scale=rs[:, b % 2, j:j + 1])
                last.then_inc(ln_done, 1)

            for b in range(4):
                ln_sqrt(0, b)
                ln_apply(0, b, first=True)
            with act.Fori(1, LN // 4) as i:
                for b in range(4):
                    ln_sqrt(i, b)
                    ln_apply(i, b)

            act.wait_ge(consts_set, 1)

            def check_tile(i, b, first=False):
                for q in range(QUARTERS):
                    if not first or q >= 2:
                        act.wait_ge(negs_checked, i * (2 * QUARTERS) + b * QUARTERS + q - 1)
                    act.wait_ge(adj_loaded[b][q], i * 16 + 16)
                    nc.scalar.activation(junk[:, q % 2], A[:, b, q * QCOLS:(q + 1) * QCOLS], ACT.Relu, scale=-1.0,
                                         accum_out=neg[:, b, q:q + 1]).then_inc(negs_checked, 1)

            def diag_tile(i, b, first=False):
                act.wait_ge(inc_ready, i * 2 + b + 1)
                if not first:
                    act.wait_ge(acc_ready, i * 2 + b - 1)
                for lo, hi in DIAG_GROUPS:
                    for s in range(lo, hi):
                        last = nc.scalar.activation(diag[:, b, s], ident[:], ACT.Copy, scale=inc[:, b, s:s + 1])
                    last.then_inc(diag_ready, 1)

            def root_tile(i, b):
                act.wait_ge(count_ready, i * 2 + b + 1)
                nc.scalar.activation(root[:, b:b + 1], cnt[:, b:b + 1], ACT.Sqrt).then_inc(root_ready, 1)

            check_tile(0, 0, first=True)
            root_tile(0, 0)
            check_tile(0, 1)
            diag_tile(0, 0, first=True)
            root_tile(0, 1)
            with act.Fori(1, TILES // 2) as i:
                check_tile(i, 0)
                diag_tile(i - 1, 1)
                root_tile(i, 0)
                check_tile(i, 1)
                diag_tile(i, 0)
                root_tile(i, 1)
            diag_tile(LAST, 1)

            act.wait_ge(list_ready, 1)
            n = act.value_load(badnu[0:1, 0:1], min_val=0, max_val=TILES)
            with act.If(n > 0):
                with act.Fori(0, n) as j:
                    act.wait_ge(d_count, j + 1)
                    nc.scalar.activation(drt[:], dcnt[:], ACT.Sqrt).then_inc(d_root, 1)

        @block.vector
        def _(dve):
            LNS = ROWS + ROWS + 1

            def ln_chunk(i, b):
                base = i * (4 * LNS) + b * LNS
                p = b % 2
                dve.wait_ge(ln_loaded[b], i * 16 + 16)
                for j in range(ROWS):
                    nc.vector.bn_stats(st[:, p, j], xin[:, b, j]).then_inc(ln_stat, 1)
                for j in range(ROWS):
                    hold(dve, ln_stat, base + j + 1)
                    nc.vector.bn_aggr(mv[:, p, j], st[:, p, j]).then_inc(ln_stat, 1)
                dve.wait_ge(ln_stat, base + 2 * ROWS)
                nc.vector.tensor_scalar(ve[:, p], mv[:, p, :, 1], EPS_NORM, None, ALU.add).then_inc(ln_var, 1)
                dve.wait_ge(ln_root, i * 4 + b + 1)
                nc.vector.reciprocal(rs[:, p], sd[:, p]).then_inc(ln_stat, 1)
                dve.wait_ge(ln_stat, base + LNS)
                nc.vector.scalar_tensor_tensor(out=nb[:, p], in0=mv[:, p, :, 0], scalar=-1.0, in1=rs[:, p],
                                               op0=ALU.mult, op1=ALU.mult).then_inc(ln_scaled, 1)

            for b in range(2):
                ln_chunk(0, b)
            for b in range(2, 4):
                dve.wait_ge(ln_done, b - 1)
                ln_chunk(0, b)
            with dve.Fori(1, LN // 4) as i:
                for b in range(4):
                    dve.wait_ge(ln_done, i * 4 + b - 1)
                    ln_chunk(i, b)

            dve.wait_ge(consts_set, 1)

            def find_values(i, b):
                for g in range(SEGS):
                    if g % SEGS_Q == 0:
                        hold(dve, adj_loaded[b][g // SEGS_Q], i * 16 + 16)
                    nc.vector.max(out=cv[:, 8 * g:8 * g + 8],
                                  in_=A[:, b, g * SEG:(g + 1) * SEG]).then_inc(vals_found, 1)

            def find_places(i, b):
                for g in range(SEGS):
                    hold(dve, vals_found, i * (2 * SEGS) + b * SEGS + g + 1)
                    nc.vector.max_index(out=ci[:, 8 * g:8 * g + 8], in_max=cv[:, 8 * g:8 * g + 8],
                                        in_values=A[:, b, g * SEG:(g + 1) * SEG]).then_inc(idx_found, 1)

            PACK = 18

            def pack_tile(i, b):
                base = i * (2 * PACK) + b * PACK
                k = [0]

                def step(ins):
                    k[0] += 1
                    ins.then_inc(pack, 1)
                    return k[0]

                def after(n):
                    hold(dve, pack, base + n)

                khf, klf = khi[:].bitcast(fp32), klo[:].bitcast(fp32)
                shf, slf = shi[:].bitcast(fp32), slo[:].bitcast(fp32)
                cvu = cv[:].bitcast(u32)
                nc.vector.tensor_scalar(cpos[:], cv[:], 0.0, 0.0, ALU.is_gt, ALU.add,
                                        accum_out=cnt[:, b:b + 1]).then_inc(count_ready, 1)
                step(nc.vector.tensor_scalar(fullf[:], cv[:, 7::8], 0.0, 0.0, ALU.is_gt, ALU.add,
                                                      accum_out=full[:]))
                dve.wait_ge(idx_found, i * (2 * SEGS) + (b + 1) * SEGS)
                s_key0 = step(nc.vector.scalar_tensor_tensor(
                    out=key0[:].rearrange("p (s e) -> p s e", e=8), in0=ci[:].rearrange("p (s e) -> p s e", e=8),
                    scalar=-65536.0, in1=segtab[:].unsqueeze(2).broadcast_to([P, SEGS, 8]),
                    op0=ALU.mult, op1=ALU.add))
                dve.wait_ge(count_ready, i * 2 + b + 1)
                after(s_key0)
                s_key = step(nc.vector.tensor_tensor(key[:], key0[:], cpos[:], ALU.mult))
                after(s_key)
                s_hi = step(nc.vector.scalar_tensor_tensor(out=khi[:], in0=cvu, scalar=16, in1=key[:],
                                                           op0=ALU.logical_shift_right, op1=ALU.bitwise_or))
                s_lo = step(nc.vector.scalar_tensor_tensor(out=klo[:], in0=cvu, scalar=65535, in1=key[:],
                                                           op0=ALU.bitwise_and, op1=ALU.bitwise_or))
                for r in range(SLOTS // 8):
                    e = slice(8 * r, 8 * r + 8)
                    after(s_hi)
                    m_hi = step(nc.vector.max(out=shf[:, e], in_=khf))
                    after(s_lo)
                    m_lo = step(nc.vector.max(out=slf[:, e], in_=klf))
                    if r < SLOTS // 8 - 1:
                        after(m_hi)
                        s_hi = step(nc.vector.match_replace(out=khf, in_to_replace=shf[:, e], in_values=khf,
                                                            imm_value=0.0))
                        after(m_lo)
                        s_lo = step(nc.vector.match_replace(out=klf, in_to_replace=slf[:, e], in_values=klf,
                                                            imm_value=0.0))
                after(m_hi)
                s_u = step(nc.vector.tensor_scalar(su[:], shi[:], 16, None, ALU.logical_shift_right))
                after(m_lo)
                s_l = step(nc.vector.tensor_scalar(sl16[:], slo[:], 65535, None, ALU.bitwise_and))
                after(s_u)
                nc.vector.tensor_scalar(idx[:, b], su[:], -1.0, float(TOP), ALU.mult, ALU.add).then_inc(cols_ready, 1)
                after(s_l)
                s_v = step(nc.vector.scalar_tensor_tensor(out=val[:, b], in0=shi[:], scalar=16, in1=sl16[:],
                                                          op0=ALU.logical_shift_left, op1=ALU.bitwise_or))
                assert s_v == PACK

            FLAG = 3

            def flag_tile(i, b):
                base = i * (2 * WEIGH) + b * WEIGH
                dve.wait_ge(negs_checked, i * (2 * QUARTERS) + (b + 1) * QUARTERS)
                nc.vector.tensor_scalar(negf[:], neg[:, b], 0.0, 0.0, ALU.not_equal, ALU.add,
                                        accum_out=negs[:]).then_inc(weigh, 1)
                nc.vector.tensor_scalar(over[:], cnt[:, b:b + 1], float(SLOTS), full[:],
                                        ALU.is_gt, ALU.add).then_inc(weigh, 1)
                nc.vector.tensor_scalar(flags[:, 0:len(EXTRA)], limits[:], cnt[:, b:b + 1], None,
                                        ALU.is_lt).then_inc(weigh, 1)
                dve.wait_ge(weigh, base + FLAG)
                nc.vector.tensor_tensor(flags[:, len(EXTRA):], over[:], negs[:], ALU.add).then_inc(flags_ready, 1)

            WEIGH = FLAG + 4

            def weigh_tile(i, b):
                base = i * (2 * WEIGH) + b * WEIGH + FLAG
                v = val[:, b].bitcast(fp32)
                dve.wait_ge(pack, i * (2 * PACK) + (b + 1) * PACK)
                nc.vector.tensor_scalar(pos[:], v, 0.0, None, ALU.is_gt).then_inc(weigh, 1)
                dve.wait_ge(root_ready, i * 2 + b + 1)
                nc.vector.tensor_scalar(rootc[:], root[:, b:b + 1], EPS_HEAD, None, ALU.max).then_inc(weigh, 1)
                dve.wait_ge(weigh, base + 2)
                nc.vector.reciprocal(head[:], rootc[:]).then_inc(weigh, 1)
                dve.wait_ge(weigh, base + 3)
                nc.vector.scalar_tensor_tensor(out=inc[:, b], in0=pos[:], scalar=head[:], in1=v,
                                               op0=ALU.mult, op1=ALU.add, accum_out=deg[:]).then_inc(inc_ready, 1)
                dve.wait_ge(inc_ready, i * 2 + b + 1)
                nc.vector.reciprocal(rdeg[:, b:b + 1], deg[:]).then_inc(weigh, 1)

            def need_tile(i, b):
                dve.wait_ge(flags_summed, i * 2 + b + 1)
                nc.vector.scalar_tensor_tensor(out=used[:, b], in0=pflag[0:1, 0:len(EXTRA)], scalar=0.0,
                                               in1=used[:, b], op0=ALU.is_gt, op1=ALU.add).then_inc(used_counted, 1)
                nc.vector.tensor_copy(need[:, b, 0:len(EXTRA)], pflag[0:1, 0:len(EXTRA)]).then_inc(need_ready, 1)
                dve.wait_ge(used_counted, i * 2 + b + 1)
                nc.vector.tensor_copy(need[:, b, len(EXTRA):], used[:, b]).then_inc(need_ready, 1)
                nc.vector.tensor_copy(bad[0:1, bass.ds(i * 2 + b, 1)],
                                      pflag[0:1, len(EXTRA):len(EXTRA) + 1]).then_inc(list_step, 1)

            def finish_tile(i, b):
                dve.wait_ge(acc_ready, i * 2 + b + 1)
                dve.wait_ge(weigh, i * (2 * WEIGH) + (b + 1) * WEIGH)
                dve.wait_ge(x_loaded[b], i * 16 + 16)
                nc.vector.scalar_tensor_tensor(out=osb[:, b], in0=acc[b][:], scalar=rdeg[:, b:b + 1],
                                               in1=xres[:, b], op0=ALU.mult, op1=ALU.add).then_inc(out_ready, 1)

            find_values(0, 0)
            find_places(0, 0)
            pack_tile(0, 0)
            flag_tile(0, 0)
            find_values(0, 1)
            weigh_tile(0, 0)
            need_tile(0, 0)
            find_places(0, 1)
            pack_tile(0, 1)
            flag_tile(0, 1)
            with dve.Fori(1, TILES // 2) as i:
                find_values(i, 0)
                weigh_tile(i - 1, 1)
                need_tile(i - 1, 1)
                find_places(i, 0)
                finish_tile(i - 1, 0)
                pack_tile(i, 0)
                flag_tile(i, 0)
                find_values(i, 1)
                weigh_tile(i, 0)
                need_tile(i, 0)
                find_places(i, 1)
                finish_tile(i - 1, 1)
                pack_tile(i, 1)
                flag_tile(i, 1)
            weigh_tile(LAST, 1)
            need_tile(LAST, 1)
            finish_tile(LAST, 0)
            finish_tile(LAST, 1)

            steps = [TILES]

            def step(ins):
                steps[0] += 1
                ins.then_inc(list_step, 1)
                dve.wait_ge(list_step, steps[0])

            dve.wait_ge(list_step, TILES)
            step(nc.vector.tensor_scalar(badk[:], bad[:], 0.0, 0.0, ALU.is_gt, ALU.add, accum_out=badn[:]))
            step(nc.vector.tensor_copy(badnu[:], badn[:]))
            step(nc.vector.tensor_tensor(badk[:], badk[:], tnum[:], ALU.mult))
            for r in range(TILES // 8):
                e = slice(8 * r, 8 * r + 8)
                step(nc.vector.max(out=badl[:, e], in_=badk[:]))
                step(nc.vector.match_replace(out=badk[:], in_to_replace=badl[:, e], in_values=badk[:],
                                             imm_value=0.0))
            nc.vector.tensor_scalar(badu[:], badl[:], -1.0, 0.0, ALU.add, ALU.max).then_inc(list_ready, 1)

            dve.wait_ge(list_ready, 1)
            n = dve.value_load(badnu[0:1, 0:1], min_val=0, max_val=TILES)
            D_STEPS = 3
            with dve.If(n > 0):
                with dve.Fori(0, n) as j:
                    dve.wait_ge(d_adj, j * 16 + 16)
                    nc.vector.tensor_scalar(A[:, 1, :], A[:, 0, :], 0.0, 0.0, ALU.is_gt, ALU.add,
                                            accum_out=dcnt[:]).then_inc(d_count, 1)
                    dve.wait_ge(d_root, j + 1)
                    nc.vector.tensor_scalar(drc[:], drt[:], EPS_HEAD, None, ALU.max).then_inc(d_step, 1)
                    dve.wait_ge(d_step, j * D_STEPS + 1)
                    nc.vector.reciprocal(dhd[:], drc[:]).then_inc(d_step, 1)
                    dve.wait_ge(d_step, j * D_STEPS + 2)
                    nc.vector.scalar_tensor_tensor(out=A[:, 0, :], in0=A[:, 1, :], scalar=dhd[:], in1=A[:, 0, :],
                                                   op0=ALU.mult, op1=ALU.add, accum_out=ddeg[:]).then_inc(d_inc, 1)
                    dve.wait_ge(d_inc, j + 1)
                    nc.vector.reciprocal(drd[:], ddeg[:]).then_inc(d_step, 1)
                    for k in range(KB):
                        dve.wait_ge(d_tr, j * KB + k + 1)
                        if k >= 2:
                            dve.wait_ge(d_mm, j * KB + k - 1)
                        nc.vector.tensor_copy(incT[:, k % 2], ptr[k % 2][:, 0:P]).then_inc(d_copied, 1)
                    dve.wait_ge(d_mm, j * KB + KB)
                    dve.wait_ge(d_step, j * D_STEPS + D_STEPS)
                    dve.wait_ge(d_x, j * 16 + 16)
                    nc.vector.scalar_tensor_tensor(out=osb[:, 0], in0=pdense[:], scalar=drd[:], in1=xres[:, 0],
                                                   op0=ALU.mult, op1=ALU.add).then_inc(d_out, 1)

        @block.tensor
        def _(pe):
            pe.wait_ge(consts_set, 1)

            def sum_flags(i, b):
                pe.wait_ge(flags_ready, i * 2 + b + 1)
                nc.tensor.matmul(pflag[0:1, 0:len(EXTRA) + 1], ones[:], flags[:],
                                 start=True, stop=True).then_inc(flags_summed, 1)

            def product(i, b, first=False):
                def add(s):
                    return nc.tensor.matmul(acc[b][:], diag[:, b, s], G[:, b, s],
                                            start=(s == 0), stop=(s == FIXED - 1))

                pe.wait_ge(diag_ready, i * (2 * len(DIAG_GROUPS)) + (b + 1) * len(DIAG_GROUPS))
                if not first:
                    pe.wait_ge(out_ready, i * 2 + b - 1)
                for s in range(FIXED - 1):
                    if s % 8 == 0:
                        pe.wait_ge(gathered[b][s // 8], i * 128 + 128)
                    add(s)
                for k, (lo, hi) in enumerate(EXTRA):
                    hold(pe, need_ready, i * 4 + b * 2 + 2)
                    v = pe.value_load(need[0:1, b, k:k + 1], min_val=0, max_val=P)
                    with pe.If(v > 0):
                        uses = pe.value_load(need[0:1, b, len(EXTRA) + k:len(EXTRA) + k + 1], min_val=1,
                                             max_val=TILES // 2)
                        pe.wait_ge(gathered[b][2 + k], uses * (16 * (hi - lo)))
                        for s in range(lo, hi):
                            add(s)
                add(FIXED - 1).then_inc(acc_ready, 1)

            for b in range(2):
                sum_flags(0, b)
                product(0, b, first=True)
            with pe.Fori(1, TILES // 2) as i:
                for b in range(2):
                    sum_flags(i, b)
                    product(i, b)

            pe.wait_ge(list_ready, 1)
            n = pe.value_load(badnu[0:1, 0:1], min_val=0, max_val=TILES)
            with pe.If(n > 0):
                with pe.Fori(0, n) as j:
                    pe.wait_ge(d_inc, j + 1)
                    for k in range(KB + 1):
                        if k < KB:
                            if k >= 2:
                                pe.wait_ge(d_copied, j * KB + k - 1)
                            nc.tensor.transpose(ptr[k % 2][:, 0:P], A[:, 0, k * P:(k + 1) * P],
                                                ident[:]).then_inc(d_tr, 1)
                        if k >= 1:
                            m = k - 1
                            pe.wait_ge(d_copied, j * KB + m + 1)
                            if m % HCH == 0:
                                pe.wait_ge(d_h[m // HCH % 2], j * (16 * NCH // 2) + 16 * (m // HCH // 2 + 1))
                            nc.tensor.matmul(pdense[:], incT[:, m % 2], G[:, m // HCH % 2, m % HCH],
                                             start=(m == 0), stop=(m == KB - 1)).then_inc(d_mm, 1)


_INS = ['x', 'adj']
_OUTS = [((8192, 512), 'float32')]


def kernel(**inputs):
    import numpy as _np
    import concourse.bacc as _bacc
    from concourse import mybir as _mybir
    from concourse.bass_utils import run_bass_kernel_spmd as _run

    nc = _bacc.Bacc("TRN2", target_bir_lowering=False, num_devices=1)
    arrays, args = {}, []
    for name in _INS:
        a = _np.ascontiguousarray(inputs[name])
        arrays[f"in_{name}_dram"] = a
        args.append(nc.dram_tensor(f"in_{name}_dram", a.shape, _mybir.dt.from_np(a.dtype), kind="ExternalInput").ap())
    for i, (shape, dtype) in enumerate(_OUTS):
        dt = _mybir.dt.from_np(_np.dtype(dtype))
        args.append(nc.dram_tensor(f"out_{i}_dram", shape, dt, kind="ExternalOutput").ap())
    add_graph_layer(nc, *args)
    r = _run(nc, [arrays], core_ids=[0])
    got = tuple(r.results[0][f"out_{i}_dram"] for i in range(len(_OUTS)))
    return got[0]
```

```python
import concourse.bass as bass
from concourse import mybir
from contextlib import ExitStack

P = 128


def add_graph_layer(nc, x, adj, out):
    fp32 = mybir.dt.float32
    bf16 = mybir.dt.bfloat16
    u32 = mybir.dt.uint32
    ALU = mybir.AluOpType
    ACT = mybir.ActivationFunctionType
    AX = mybir.AxisListType

    N, D = x.shape
    TILES = N // P
    EPS_NORM = 1e-5
    EPS_HEAD = 1e-12

    SEGS = 8
    SEG = N // SEGS
    CAND = 8 * SEGS
    QUARTERS = 4
    QCOLS = N // QUARTERS
    SEGS_Q = SEGS // QUARTERS
    SLOTS = 24
    BIAS = 128
    TOP = BIAS + N - 1
    OWN = 11
    SPILL = SLOTS - OWN
    FAR = 1000.0
    GROUPS = [(0, 6), (6, OWN)]

    ROWS = 4
    LN = N // (P * ROWS)
    KB = N // P
    HCH = 8
    NCH = KB // HCH

    x_ln = x.rearrange("(c p j) d -> c p j d", p=P, j=ROWS)
    x_t = x.rearrange("(t p) d -> t p d", p=P)
    out_t = out.rearrange("(t p) d -> t p d", p=P)
    adj_t = adj.rearrange("(t p) n -> t p n", p=P)

    ctx = ExitStack()
    with ctx:
        def sb(name, shape, dt):
            return ctx.enter_context(nc.sbuf_tensor(name, shape, dt))

        def sem(name):
            return ctx.enter_context(nc.semaphore(name))

        h = nc.dram_tensor("h_scratch", [N, D], fp32, kind="Internal").ap()
        h_ln = h.rearrange("(c p j) d -> c p j d", p=P, j=ROWS)
        h_blk = h.rearrange("(c k p) d -> c p k d", p=P, k=HCH)

        A = sb("adj_tile", [P, 2, N], fp32)
        G = sb("gathered", [P, 2, OWN + 1, D], fp32)
        diag = sb("diag", [P, 2, OWN, P], fp32)
        ident = sb("ident", [P, P], fp32)
        ones = sb("ones", [P, 1], fp32)
        junk = sb("junk", [P, 2, QCOLS], bf16)
        xres = sb("x_residual", [P, 2, D], fp32)
        osb = sb("out_tile", [P, 2, D], fp32)
        cv = sb("cand_value", [P, CAND], fp32)
        ci = sb("cand_index", [P, CAND], u32)
        cpos = sb("cand_positive", [P, CAND], fp32)
        segtab = sb("segment_key", [P, SEGS], fp32)
        key0 = sb("key0", [P, CAND], u32)
        key = sb("key", [P, CAND], u32)
        khi = sb("key_high", [P, CAND], u32)
        klo = sb("key_low", [P, CAND], u32)
        shi = sb("sorted_high", [P, SLOTS], u32)
        slo = sb("sorted_low", [P, SLOTS], u32)
        su = sb("slot_rank", [P, SLOTS], u32)
        sl16 = sb("slot_low16", [P, SLOTS], u32)
        idx = sb("slot_column", [P, 2, SLOTS], u32)
        val = sb("slot_value", [P, 2, SLOTS], u32)
        pos = sb("slot_positive", [P, SLOTS], fp32)
        inc = sb("slot_inc", [P, 2, SLOTS], fp32)
        cnt = sb("count", [P, 2], fp32)
        full = sb("full_segments", [P, 1], fp32)
        fullf = sb("full_flags", [P, SEGS], fp32)
        neg = sb("negatives", [P, 2, QUARTERS], fp32)
        negf = sb("negative_flags", [P, QUARTERS], fp32)
        negs = sb("negative_count", [P, 1], fp32)
        over = sb("overfull", [P, 1], fp32)
        slotno = sb("slot_number", [P, SPILL], fp32)
        spillno = sb("spill_number", [P, SPILL], fp32)
        lane = sb("lane_number", [P, P], fp32)
        tri = sb("lanes_before", [P, P], fp32)
        spilln = sb("spill_count", [P, 1], fp32)
        miss = sb("spill_miss", [P, SPILL], fp32)
        place = sb("spill_place", [P, SPILL], fp32)
        onehot = sb("spill_onehot", [P, SPILL, P], fp32)
        pay = sb("spill_payload", [P, SPILL, 3], fp32)
        spidx = sb("spill_column", [P, 2], u32)
        sprow = sb("spill_row_inc", [P, 2], fp32)
        W = sb("spill_matrix", [P, 2, P], fp32)
        late = sb("spill_overfull", [P, 1], fp32)
        root = sb("root", [P, 2], fp32)
        rootc = sb("root_clamped", [P, 1], fp32)
        head = sb("head", [P, 1], fp32)
        deg = sb("degree", [P, 1], fp32)
        rdeg = sb("inv_degree", [P, 2], fp32)
        tnum = sb("tile_number", [1, TILES], fp32)
        badm = sb("bad_rows", [P, TILES], fp32)
        badk = sb("bad_key", [1, TILES], fp32)
        badl = sb("bad_list", [1, TILES], fp32)
        badu = sb("bad_list_int", [1, TILES], u32)
        badn = sb("bad_number", [1, 1], fp32)
        badnu = sb("bad_number_int", [1, 1], u32)
        xin = sb("ln_x", [P, 4, ROWS, D], fp32)
        hst = sb("ln_h", [P, 2, ROWS, D], fp32)
        st = sb("ln_stats", [P, 2, ROWS, 6], fp32)
        mv = sb("ln_mean_var", [P, 2, ROWS, 2], fp32)
        ve = sb("ln_var_eps", [P, 2, ROWS], fp32)
        sd = sb("ln_std", [P, 2, ROWS], fp32)
        rs = sb("ln_rstd", [P, 2, ROWS], fp32)
        nb = sb("ln_bias", [P, 2, ROWS], fp32)
        incT = sb("inc_T", [P, 2, P], fp32)
        dcnt = sb("dense_count", [P, 1], fp32)
        drt = sb("dense_root", [P, 1], fp32)
        drc = sb("dense_root_clamped", [P, 1], fp32)
        dhd = sb("dense_head", [P, 1], fp32)
        ddeg = sb("dense_degree", [P, 1], fp32)
        drd = sb("dense_inv_degree", [P, 1], fp32)

        acc = [ctx.enter_context(nc.psum_tensor(f"acc{b}", [P, D], fp32)) for b in range(2)]
        poff = ctx.enter_context(nc.psum_tensor("poff", [P, 512], fp32))
        pspill = ctx.enter_context(nc.psum_tensor("pspill", [P, 512], fp32))
        ptr = [ctx.enter_context(nc.psum_tensor(f"ptr{b}", [P, 512], fp32)) for b in range(2)]
        pdense = ctx.enter_context(nc.psum_tensor("pdense", [P, D], fp32))

        const_step = sem("const_step")
        passed = sem("passed")
        consts_set = sem("consts_set")
        zeroed = sem("zeroed")
        ln_loaded = [sem(f"ln_loaded{b}") for b in range(4)]
        ln_stat = sem("ln_stat")
        ln_var = sem("ln_var")
        ln_root = sem("ln_root")
        ln_scaled = sem("ln_scaled")
        ln_done = sem("ln_done")
        h_stored = [sem(f"h_stored{b}") for b in range(4)]
        adj_loaded = [[sem(f"adj_loaded{b}{q}") for q in range(QUARTERS)] for b in range(2)]
        x_loaded = [sem(f"x_loaded{b}") for b in range(2)]
        negs_checked = sem("negs_checked")
        vals_found = sem("vals_found")
        idx_found = sem("idx_found")
        pack = sem("pack")
        cols_ready = sem("cols_ready")
        count_ready = sem("count_ready")
        spill_counted = sem("spill_counted")
        spill_offset = sem("spill_offset")
        flag = sem("flag")
        place_step = sem("place_step")
        place_ready = sem("place_ready")
        pay_ready = sem("pay_ready")
        onehot_ready = sem("onehot_ready")
        spill_moved = sem("spill_moved")
        spidx_ready = sem("spidx_ready")
        sprow_ready = sem("sprow_ready")
        w_ready = sem("w_ready")
        bad_marked = sem("bad_marked")
        bad_summed = sem("bad_summed")
        root_ready = sem("root_ready")
        weigh = sem("weigh")
        inc_ready = sem("inc_ready")
        diag_ready = sem("diag_ready")
        gathered = [[sem(f"gathered{b}{g}") for g in range(len(GROUPS) + 1)] for b in range(2)]
        acc_ready = sem("acc_ready")
        out_ready = sem("out_ready")
        out_stored = [sem(f"out_stored{b}") for b in range(2)]
        list_step = sem("list_step")
        list_ready = sem("list_ready")
        d_adj = sem("d_adj")
        d_x = sem("d_x")
        d_h = [sem(f"d_h{b}") for b in range(2)]
        d_step = sem("d_step")
        d_count = sem("d_count")
        d_root = sem("d_root")
        d_inc = sem("d_inc")
        d_tr = sem("d_tr")
        d_copied = sem("d_copied")
        d_mm = sem("d_mm")
        d_out = sem("d_out")
        d_stored = sem("d_stored")

        def hold(eng, signal, value):
            eng.wait_ge(signal, value)
            eng.sem_inc(passed, 1)

        block = ctx.enter_context(nc.Block())
        LAST = TILES // 2 - 1

        @block.sync
        def _(sp):
            def ln_load(i, b):
                sp.dma_start(xin[:, b], x_ln[i * 4 + b]).then_inc(ln_loaded[b], 16)

            def ln_store(i, b):
                sp.wait_ge(ln_done, i * 4 + b + 1)
                sp.dma_start(h_ln[i * 4 + b], hst[:, b % 2]).then_inc(h_stored[b], 16)

            def load_tile(i, b, first=False):
                for q in range(QUARTERS):
                    if not first:
                        hold(sp, idx_found, i * (2 * SEGS) + (b - 2) * SEGS + (q + 1) * SEGS_Q)
                        sp.wait_ge(negs_checked, i * (2 * QUARTERS) + (b - 2) * QUARTERS + q + 1)
                    sp.dma_start(A[:, b, q * QCOLS:(q + 1) * QCOLS],
                                 adj_t[i * 2 + b, :, q * QCOLS:(q + 1) * QCOLS]).then_inc(adj_loaded[b][q], 16)

            def load_x(i, b):
                sp.dma_start(xres[:, b], x_t[i * 2 + b]).then_inc(x_loaded[b], 16)

            def store_tile(i, b):
                hold(sp, out_ready, i * 2 + b + 1)
                sp.dma_start(out_t[i * 2 + b], osb[:, b]).then_inc(out_stored[b], 16)

            for b in range(4):
                ln_load(0, b)
            for b in range(2):
                load_tile(0, b, first=True)
                load_x(0, b)
            with sp.Fori(1, LN // 4) as i:
                for b in range(4):
                    ln_store(i - 1, b)
                    ln_load(i, b)
            for b in range(4):
                ln_store(LN // 4 - 1, b)

            for b in range(2):
                load_tile(1, b)
            with sp.Fori(2, TILES // 2) as i:
                for b in range(2):
                    load_tile(i, b)
                    store_tile(i - 2, b)
                    hold(sp, out_stored[b], i * 16 - 16)
                    load_x(i - 1, b)
            for b in range(2):
                store_tile(LAST - 1, b)
                sp.wait_ge(out_stored[b], 16 * (TILES // 2 - 1))
                load_x(LAST, b)
            for b in range(2):
                store_tile(LAST, b)
            for b in range(2):
                sp.wait_ge(out_stored[b], 16 * (TILES // 2))

            sp.wait_ge(list_ready, 1)
            n = sp.value_load(badnu[0:1, 0:1], min_val=0, max_val=TILES)
            with sp.If(n > 0):
                with sp.Fori(0, n) as j:
                    t = sp.value_load(badu[0:1, bass.ds(j, 1)], min_val=0, max_val=TILES - 1)
                    sp.dma_start(A[:, 0, :], adj_t[t]).then_inc(d_adj, 16)
                    sp.dma_start(xres[:, 0], x_t[t]).then_inc(d_x, 16)
                    for c in range(NCH):
                        if c >= 2:
                            sp.wait_ge(d_mm, j * KB + (c - 1) * HCH)
                        sp.dma_start(G[:, c % 2, 0:HCH, :], h_blk[c]).then_inc(d_h[c % 2], 16)
                    sp.wait_ge(d_out, j + 1)
                    sp.dma_start(out_t[t], osb[:, 0]).then_inc(d_stored, 16)
                    hold(sp, d_stored, j * 16 + 16)

        @block.gpsimd
        def _(pool):
            steps = [0]

            def step(ins):
                steps[0] += 1
                ins.then_inc(const_step, 1)
                pool.wait_ge(const_step, steps[0])

            step(nc.gpsimd.memset(ident[:], 0.0))
            step(nc.gpsimd.affine_select(out=ident[:], in_=ident[:], compare_op=ALU.not_equal, fill=1.0,
                                         base=0, pattern=[[-1, P]], channel_multiplier=1))
            step(nc.gpsimd.memset(ones[:], 1.0))
            step(nc.gpsimd.iota(tnum[:], pattern=[[1, TILES]], base=1, channel_multiplier=0,
                                allow_small_or_imprecise_dtypes=True))
            for s in range(SEGS):
                step(nc.gpsimd.memset(segtab[:, s:s + 1], float((TOP - SEG * s) * 65536)))
            step(nc.gpsimd.iota(slotno[:], pattern=[[1, SPILL]], base=OWN, channel_multiplier=0,
                                allow_small_or_imprecise_dtypes=True))
            step(nc.gpsimd.iota(spillno[:], pattern=[[1, SPILL]], base=0, channel_multiplier=0,
                                allow_small_or_imprecise_dtypes=True))
            step(nc.gpsimd.iota(lane[:], pattern=[[1, P]], base=0, channel_multiplier=0,
                                allow_small_or_imprecise_dtypes=True))
            step(nc.gpsimd.iota(pay[:, :, 1], pattern=[[0, SPILL]], base=0, channel_multiplier=1,
                                allow_small_or_imprecise_dtypes=True))
            step(nc.gpsimd.memset(tri[:], 1.0))
            step(nc.gpsimd.affine_select(out=tri[:], in_=tri[:], compare_op=ALU.is_gt, fill=0.0,
                                         base=0, pattern=[[1, P]], channel_multiplier=-1))
            pool.sem_inc(consts_set, 1)
            nc.gpsimd.memset(G[:, 0], 0.0).then_inc(zeroed, 1)
            nc.gpsimd.memset(G[:, 1], 0.0).then_inc(zeroed, 1)

            pool.wait_ge(zeroed, 2)
            for b in range(4):
                pool.wait_ge(h_stored[b], 16 * (LN // 4))

            def gather(b, s, column, done):
                nc.gpsimd.indirect_dma_start(
                    out=G[:, b, s, :], out_offset=None, in_=h[:, :],
                    in_offset=bass.IndirectOffsetOnAxis(ap=column, axis=0),
                    bounds_check=N - 1, oob_is_err=False).then_inc(done, 16)

            def gather_tile(i, b, first=False):
                if not first:
                    pool.wait_ge(acc_ready, i * 2 + b - 1)
                hold(pool, cols_ready, i * 2 + b + 1)
                for s in range(OWN):
                    if s == 3:
                        hold(pool, place_ready, i * 2 + b + 1)
                        for k in range(SPILL):
                            last = nc.gpsimd.tensor_scalar(onehot[:, k], lane[:], place[:, k:k + 1], None,
                                                           ALU.is_equal)
                        last.then_inc(onehot_ready, 1)
                    gather(b, s, idx[:, b, s:s + 1], gathered[b][0 if s < GROUPS[0][1] else 1])
                hold(pool, spidx_ready, i * 2 + b + 1)
                gather(b, OWN, spidx[:, b:b + 1], gathered[b][2])

            for b in range(2):
                gather_tile(0, b, first=True)
            with pool.Fori(1, TILES // 2) as i:
                for b in range(2):
                    gather_tile(i, b)

        @block.scalar
        def _(act):
            def ln_sqrt(i, b):
                act.wait_ge(ln_var, i * 4 + b + 1)
                nc.scalar.activation(sd[:, b % 2], ve[:, b % 2], ACT.Sqrt).then_inc(ln_root, 1)

            def ln_apply(i, b, first=False):
                act.wait_ge(ln_scaled, i * 4 + b + 1)
                if not first or b >= 2:
                    act.wait_ge(h_stored[(b + 2) % 4], i * 16 + 16 * (b >= 2))
                for j in range(ROWS):
                    last = nc.scalar.activation(hst[:, b % 2, j], xin[:, b, j], ACT.Relu,
                                                bias=nb[:, b % 2, j:j + 1], scale=rs[:, b % 2, j:j + 1])
                last.then_inc(ln_done, 1)

            for b in range(4):
                ln_sqrt(0, b)
                ln_apply(0, b, first=True)
            with act.Fori(1, LN // 4) as i:
                for b in range(4):
                    ln_sqrt(i, b)
                    ln_apply(i, b)

            act.wait_ge(consts_set, 1)

            def check_tile(i, b, first=False):
                for q in range(QUARTERS):
                    if not first or q >= 2:
                        act.wait_ge(negs_checked, i * (2 * QUARTERS) + b * QUARTERS + q - 1)
                    act.wait_ge(adj_loaded[b][q], i * 16 + 16)
                    nc.scalar.activation(junk[:, q % 2], A[:, b, q * QCOLS:(q + 1) * QCOLS], ACT.Relu, scale=-1.0,
                                         accum_out=neg[:, b, q:q + 1]).then_inc(negs_checked, 1)

            def diag_tile(i, b, first=False):
                act.wait_ge(inc_ready, i * 2 + b + 1)
                if not first:
                    act.wait_ge(acc_ready, i * 2 + b - 1)
                for lo, hi in GROUPS:
                    for s in range(lo, hi):
                        last = nc.scalar.activation(diag[:, b, s], ident[:], ACT.Copy, scale=inc[:, b, s:s + 1])
                    last.then_inc(diag_ready, 1)

            def root_tile(i, b):
                act.wait_ge(count_ready, i * 2 + b + 1)
                nc.scalar.activation(root[:, b:b + 1], cnt[:, b:b + 1], ACT.Sqrt).then_inc(root_ready, 1)

            check_tile(0, 0, first=True)
            root_tile(0, 0)
            check_tile(0, 1)
            diag_tile(0, 0, first=True)
            root_tile(0, 1)
            with act.Fori(1, TILES // 2) as i:
                check_tile(i, 0)
                diag_tile(i - 1, 1)
                root_tile(i, 0)
                check_tile(i, 1)
                diag_tile(i, 0)
                root_tile(i, 1)
            diag_tile(LAST, 1)

            act.wait_ge(list_ready, 1)
            n = act.value_load(badnu[0:1, 0:1], min_val=0, max_val=TILES)
            with act.If(n > 0):
                with act.Fori(0, n) as j:
                    act.wait_ge(d_count, j + 1)
                    nc.scalar.activation(drt[:], dcnt[:], ACT.Sqrt).then_inc(d_root, 1)

        @block.vector
        def _(dve):
            LNS = ROWS + ROWS + 1

            def ln_chunk(i, b):
                base = i * (4 * LNS) + b * LNS
                p = b % 2
                dve.wait_ge(ln_loaded[b], i * 16 + 16)
                for j in range(ROWS):
                    nc.vector.bn_stats(st[:, p, j], xin[:, b, j]).then_inc(ln_stat, 1)
                for j in range(ROWS):
                    hold(dve, ln_stat, base + j + 1)
                    nc.vector.bn_aggr(mv[:, p, j], st[:, p, j]).then_inc(ln_stat, 1)
                dve.wait_ge(ln_stat, base + 2 * ROWS)
                nc.vector.tensor_scalar(ve[:, p], mv[:, p, :, 1], EPS_NORM, None, ALU.add).then_inc(ln_var, 1)
                dve.wait_ge(ln_root, i * 4 + b + 1)
                nc.vector.reciprocal(rs[:, p], sd[:, p]).then_inc(ln_stat, 1)
                dve.wait_ge(ln_stat, base + LNS)
                nc.vector.scalar_tensor_tensor(out=nb[:, p], in0=mv[:, p, :, 0], scalar=-1.0, in1=rs[:, p],
                                               op0=ALU.mult, op1=ALU.mult).then_inc(ln_scaled, 1)

            for b in range(2):
                ln_chunk(0, b)
            for b in range(2, 4):
                dve.wait_ge(ln_done, b - 1)
                ln_chunk(0, b)
            with dve.Fori(1, LN // 4) as i:
                for b in range(4):
                    dve.wait_ge(ln_done, i * 4 + b - 1)
                    ln_chunk(i, b)

            dve.wait_ge(consts_set, 1)

            def find_values(i, b, lo, hi):
                for g in range(lo, hi):
                    if g % SEGS_Q == 0:
                        hold(dve, adj_loaded[b][g // SEGS_Q], i * 16 + 16)
                    nc.vector.max(out=cv[:, 8 * g:8 * g + 8],
                                  in_=A[:, b, g * SEG:(g + 1) * SEG]).then_inc(vals_found, 1)

            def find_places(i, b):
                for g in range(SEGS):
                    hold(dve, vals_found, i * (2 * SEGS) + b * SEGS + g + 1)
                    nc.vector.max_index(out=ci[:, 8 * g:8 * g + 8], in_max=cv[:, 8 * g:8 * g + 8],
                                        in_values=A[:, b, g * SEG:(g + 1) * SEG]).then_inc(idx_found, 1)

            PACK = 18

            def pack_tile(i, b):
                base = i * (2 * PACK) + b * PACK
                k = [0]

                def step(ins):
                    k[0] += 1
                    ins.then_inc(pack, 1)
                    return k[0]

                def after(n):
                    hold(dve, pack, base + n)

                khf, klf = khi[:].bitcast(fp32), klo[:].bitcast(fp32)
                shf, slf = shi[:].bitcast(fp32), slo[:].bitcast(fp32)
                cvu = cv[:].bitcast(u32)
                nc.vector.tensor_scalar(cpos[:], cv[:], 0.0, 0.0, ALU.is_gt, ALU.add,
                                        accum_out=cnt[:, b:b + 1]).then_inc(count_ready, 1)
                step(nc.vector.tensor_scalar(fullf[:], cv[:, 7::8], 0.0, 0.0, ALU.is_gt, ALU.add,
                                                      accum_out=full[:]))
                dve.wait_ge(idx_found, i * (2 * SEGS) + (b + 1) * SEGS)
                s_key0 = step(nc.vector.scalar_tensor_tensor(
                    out=key0[:].rearrange("p (s e) -> p s e", e=8), in0=ci[:].rearrange("p (s e) -> p s e", e=8),
                    scalar=-65536.0, in1=segtab[:].unsqueeze(2).broadcast_to([P, SEGS, 8]),
                    op0=ALU.mult, op1=ALU.add))
                dve.wait_ge(count_ready, i * 2 + b + 1)
                after(s_key0)
                nc.vector.tensor_scalar(spilln[:], cnt[:, b:b + 1], -float(OWN), 0.0, ALU.add,
                                        ALU.max).then_inc(spill_counted, 1)
                s_key = step(nc.vector.tensor_tensor(key[:], key0[:], cpos[:], ALU.mult))
                after(s_key)
                s_hi = step(nc.vector.scalar_tensor_tensor(out=khi[:], in0=cvu, scalar=16, in1=key[:],
                                                           op0=ALU.logical_shift_right, op1=ALU.bitwise_or))
                s_lo = step(nc.vector.scalar_tensor_tensor(out=klo[:], in0=cvu, scalar=65535, in1=key[:],
                                                           op0=ALU.bitwise_and, op1=ALU.bitwise_or))
                for r in range(SLOTS // 8):
                    e = slice(8 * r, 8 * r + 8)
                    after(s_hi)
                    m_hi = step(nc.vector.max(out=shf[:, e], in_=khf))
                    after(s_lo)
                    m_lo = step(nc.vector.max(out=slf[:, e], in_=klf))
                    if r < SLOTS // 8 - 1:
                        after(m_hi)
                        s_hi = step(nc.vector.match_replace(out=khf, in_to_replace=shf[:, e], in_values=khf,
                                                            imm_value=0.0))
                        after(m_lo)
                        s_lo = step(nc.vector.match_replace(out=klf, in_to_replace=slf[:, e], in_values=klf,
                                                            imm_value=0.0))
                after(m_hi)
                s_u = step(nc.vector.tensor_scalar(su[:], shi[:], 16, None, ALU.logical_shift_right))
                after(m_lo)
                s_l = step(nc.vector.tensor_scalar(sl16[:], slo[:], 65535, None, ALU.bitwise_and))
                after(s_u)
                nc.vector.tensor_scalar(idx[:, b], su[:], -1.0, float(TOP), ALU.mult, ALU.add).then_inc(cols_ready, 1)
                after(s_l)
                s_v = step(nc.vector.scalar_tensor_tensor(out=val[:, b], in0=shi[:], scalar=16, in1=sl16[:],
                                                          op0=ALU.logical_shift_left, op1=ALU.bitwise_or))
                assert s_v == PACK

            WEIGH = 4

            def weigh_tile(i, b):
                base = i * (2 * WEIGH) + b * WEIGH
                v = val[:, b].bitcast(fp32)
                dve.wait_ge(pack, i * (2 * PACK) + (b + 1) * PACK)
                nc.vector.tensor_scalar(pos[:], v, 0.0, None, ALU.is_gt).then_inc(weigh, 1)
                dve.wait_ge(root_ready, i * 2 + b + 1)
                nc.vector.tensor_scalar(rootc[:], root[:, b:b + 1], EPS_HEAD, None, ALU.max).then_inc(weigh, 1)
                dve.wait_ge(weigh, base + 2)
                nc.vector.reciprocal(head[:], rootc[:]).then_inc(weigh, 1)
                dve.wait_ge(weigh, base + 3)
                nc.vector.scalar_tensor_tensor(out=inc[:, b], in0=pos[:], scalar=head[:], in1=v,
                                               op0=ALU.mult, op1=ALU.add, accum_out=deg[:]).then_inc(inc_ready, 1)
                dve.wait_ge(inc_ready, i * 2 + b + 1)
                nc.vector.reciprocal(rdeg[:, b:b + 1], deg[:]).then_inc(weigh, 1)

            def place_tile(i, b):
                dve.wait_ge(pack, i * (2 * PACK) + (b + 1) * PACK)
                nc.vector.tensor_scalar(miss[:], slotno[:], cnt[:, b:b + 1], FAR,
                                        ALU.is_ge, ALU.mult).then_inc(place_step, 1)
                dve.wait_ge(spill_offset, i * 2 + b + 1)
                dve.wait_ge(place_step, i * 2 + b + 1)
                nc.vector.scalar_tensor_tensor(out=place[:], in0=spillno[:], scalar=poff[:, 0:1], in1=miss[:],
                                               op0=ALU.add, op1=ALU.add).then_inc(place_ready, 1)
                dve.wait_ge(cols_ready, i * 2 + b + 1)
                nc.vector.tensor_copy(pay[:, :, 0], idx[:, b, OWN:]).then_inc(pay_ready, 1)

            FLAG = 3

            def flag_tile(i, b):
                dve.wait_ge(negs_checked, i * (2 * QUARTERS) + (b + 1) * QUARTERS)
                nc.vector.tensor_scalar(negf[:], neg[:, b], 0.0, 0.0, ALU.not_equal, ALU.add,
                                        accum_out=negs[:]).then_inc(flag, 1)
                nc.vector.tensor_scalar(over[:], cnt[:, b:b + 1], float(SLOTS), full[:],
                                        ALU.is_gt, ALU.add).then_inc(flag, 1)
                nc.vector.tensor_scalar(late[:], spilln[:], poff[:, 0:1], float(P) + 0.5,
                                        ALU.add, ALU.is_gt).then_inc(flag, 1)
                dve.wait_ge(flag, i * (2 * FLAG) + (b + 1) * FLAG)
                nc.vector.scalar_tensor_tensor(out=badm[:, bass.ds(i * 2 + b, 1)], in0=over[:], scalar=negs[:],
                                               in1=late[:], op0=ALU.add, op1=ALU.add).then_inc(bad_marked, 1)

            def pay_tile(i, b):
                dve.wait_ge(inc_ready, i * 2 + b + 1)
                nc.vector.tensor_copy(pay[:, :, 2], inc[:, b, OWN:]).then_inc(pay_ready, 1)

            def spill_tile(i, b):
                dve.wait_ge(spill_moved, i * 2 + b + 1)
                nc.vector.tensor_copy(spidx[:, b:b + 1], pspill[:, 0:1]).then_inc(spidx_ready, 1)
                nc.vector.tensor_copy(sprow[:], pspill[:, 1:3]).then_inc(sprow_ready, 1)
                dve.wait_ge(sprow_ready, i * 2 + b + 1)
                nc.vector.tensor_scalar(W[:, b], lane[:], sprow[:, 0:1], sprow[:, 1:2],
                                        ALU.is_equal, ALU.mult).then_inc(w_ready, 1)

            def finish_tile(i, b):
                dve.wait_ge(acc_ready, i * 2 + b + 1)
                dve.wait_ge(weigh, i * (2 * WEIGH) + (b + 1) * WEIGH)
                dve.wait_ge(x_loaded[b], i * 16 + 16)
                nc.vector.scalar_tensor_tensor(out=osb[:, b], in0=acc[b][:], scalar=rdeg[:, b:b + 1],
                                               in1=xres[:, b], op0=ALU.mult, op1=ALU.add).then_inc(out_ready, 1)

            def middle(i, b):
                weigh_tile(i, b)
                place_tile(i, b)
                pay_tile(i, b)
                flag_tile(i, b)

            FIRST = 2
            find_values(0, 0, 0, SEGS)
            find_places(0, 0)
            pack_tile(0, 0)
            find_values(0, 1, 0, FIRST)
            middle(0, 0)
            find_values(0, 1, FIRST, SEGS)
            find_places(0, 1)
            spill_tile(0, 0)
            pack_tile(0, 1)
            with dve.Fori(1, TILES // 2) as i:
                for b in range(2):
                    t1 = (i - 1, 1) if b == 0 else (i, 0)
                    find_values(i, b, 0, FIRST)
                    middle(*t1)
                    find_values(i, b, FIRST, SEGS)
                    find_places(i, b)
                    spill_tile(*t1)
                    finish_tile(i - 1, b)
                    pack_tile(i, b)
            middle(LAST, 1)
            spill_tile(LAST, 1)
            finish_tile(LAST, 0)
            finish_tile(LAST, 1)

            steps = [0]

            def step(ins):
                steps[0] += 1
                ins.then_inc(list_step, 1)
                dve.wait_ge(list_step, steps[0])

            dve.wait_ge(bad_summed, 1)
            step(nc.vector.tensor_scalar(badk[:], poff[0:1, 0:TILES], 0.0, 0.0, ALU.is_gt, ALU.add,
                                         accum_out=badn[:]))
            step(nc.vector.tensor_copy(badnu[:], badn[:]))
            step(nc.vector.tensor_tensor(badk[:], badk[:], tnum[:], ALU.mult))
            for r in range(TILES // 8):
                e = slice(8 * r, 8 * r + 8)
                step(nc.vector.max(out=badl[:, e], in_=badk[:]))
                step(nc.vector.match_replace(out=badk[:], in_to_replace=badl[:, e], in_values=badk[:],
                                             imm_value=0.0))
            nc.vector.tensor_scalar(badu[:], badl[:], -1.0, 0.0, ALU.add, ALU.max).then_inc(list_ready, 1)

            dve.wait_ge(list_ready, 1)
            n = dve.value_load(badnu[0:1, 0:1], min_val=0, max_val=TILES)
            D_STEPS = 3
            with dve.If(n > 0):
                with dve.Fori(0, n) as j:
                    dve.wait_ge(d_adj, j * 16 + 16)
                    nc.vector.tensor_scalar(A[:, 1, :], A[:, 0, :], 0.0, 0.0, ALU.is_gt, ALU.add,
                                            accum_out=dcnt[:]).then_inc(d_count, 1)
                    dve.wait_ge(d_root, j + 1)
                    nc.vector.tensor_scalar(drc[:], drt[:], EPS_HEAD, None, ALU.max).then_inc(d_step, 1)
                    dve.wait_ge(d_step, j * D_STEPS + 1)
                    nc.vector.reciprocal(dhd[:], drc[:]).then_inc(d_step, 1)
                    dve.wait_ge(d_step, j * D_STEPS + 2)
                    nc.vector.scalar_tensor_tensor(out=A[:, 0, :], in0=A[:, 1, :], scalar=dhd[:], in1=A[:, 0, :],
                                                   op0=ALU.mult, op1=ALU.add, accum_out=ddeg[:]).then_inc(d_inc, 1)
                    dve.wait_ge(d_inc, j + 1)
                    nc.vector.reciprocal(drd[:], ddeg[:]).then_inc(d_step, 1)
                    for k in range(KB):
                        dve.wait_ge(d_tr, j * KB + k + 1)
                        if k >= 2:
                            dve.wait_ge(d_mm, j * KB + k - 1)
                        nc.vector.tensor_copy(incT[:, k % 2], ptr[k % 2][:, 0:P]).then_inc(d_copied, 1)
                    dve.wait_ge(d_mm, j * KB + KB)
                    dve.wait_ge(d_step, j * D_STEPS + D_STEPS)
                    dve.wait_ge(d_x, j * 16 + 16)
                    nc.vector.scalar_tensor_tensor(out=osb[:, 0], in0=pdense[:], scalar=drd[:], in1=xres[:, 0],
                                                   op0=ALU.mult, op1=ALU.add).then_inc(d_out, 1)

        @block.tensor
        def _(pe):
            pe.wait_ge(consts_set, 1)

            def offsets(i, b):
                pe.wait_ge(spill_counted, i * 2 + b + 1)
                nc.tensor.matmul(poff[:, 0:1], tri[:], spilln[:], start=True, stop=True).then_inc(spill_offset, 1)

            def move_spill(i, b):
                pe.wait_ge(pay_ready, i * 4 + b * 2 + 2)
                pe.wait_ge(onehot_ready, i * 2 + b + 1)
                for k in range(SPILL):
                    last = nc.tensor.matmul(pspill[:, 0:3], onehot[:, k], pay[:, k], start=(k == 0),
                                            stop=(k == SPILL - 1))
                last.then_inc(spill_moved, 1)

            def product(i, b, first=False):
                if not first:
                    pe.wait_ge(out_ready, i * 2 + b - 1)
                for g, (lo, hi) in enumerate(GROUPS):
                    pe.wait_ge(diag_ready, i * (2 * len(GROUPS)) + b * len(GROUPS) + g + 1)
                    pe.wait_ge(gathered[b][g], i * (16 * (hi - lo)) + 16 * (hi - lo))
                    for s in range(lo, hi):
                        nc.tensor.matmul(acc[b][:], diag[:, b, s], G[:, b, s], start=(s == 0), stop=False)
                pe.wait_ge(w_ready, i * 2 + b + 1)
                pe.wait_ge(gathered[b][len(GROUPS)], i * 16 + 16)
                nc.tensor.matmul(acc[b][:], W[:, b], G[:, b, OWN], start=False, stop=True).then_inc(acc_ready, 1)

            offsets(0, 0)
            move_spill(0, 0)
            offsets(0, 1)
            product(0, 0, first=True)
            move_spill(0, 1)
            offsets(1, 0)
            product(0, 1, first=True)
            move_spill(1, 0)
            offsets(1, 1)
            product(1, 0)
            move_spill(1, 1)
            with pe.Fori(2, TILES // 2) as i:
                offsets(i, 0)
                product(i - 1, 1)
                move_spill(i, 0)
                offsets(i, 1)
                product(i, 0)
                move_spill(i, 1)
            product(LAST, 1)
            pe.wait_ge(bad_marked, TILES)
            nc.tensor.matmul(poff[0:1, 0:TILES], ones[:], badm[:], start=True, stop=True).then_inc(bad_summed, 1)

            pe.wait_ge(list_ready, 1)
            n = pe.value_load(badnu[0:1, 0:1], min_val=0, max_val=TILES)
            with pe.If(n > 0):
                with pe.Fori(0, n) as j:
                    pe.wait_ge(d_inc, j + 1)
                    for k in range(KB + 1):
                        if k < KB:
                            if k >= 2:
                                pe.wait_ge(d_copied, j * KB + k - 1)
                            nc.tensor.transpose(ptr[k % 2][:, 0:P], A[:, 0, k * P:(k + 1) * P],
                                                ident[:]).then_inc(d_tr, 1)
                        if k >= 1:
                            m = k - 1
                            pe.wait_ge(d_copied, j * KB + m + 1)
                            if m % HCH == 0:
                                pe.wait_ge(d_h[m // HCH % 2], j * (16 * NCH // 2) + 16 * (m // HCH // 2 + 1))
                            nc.tensor.matmul(pdense[:], incT[:, m % 2], G[:, m // HCH % 2, m % HCH],
                                             start=(m == 0), stop=(m == KB - 1)).then_inc(d_mm, 1)


_INS = ['x', 'adj']
_OUTS = [((8192, 512), 'float32')]


def kernel(**inputs):
    import numpy as _np
    import concourse.bacc as _bacc
    from concourse import mybir as _mybir
    from concourse.bass_utils import run_bass_kernel_spmd as _run

    nc = _bacc.Bacc("TRN2", target_bir_lowering=False, num_devices=1)
    arrays, args = {}, []
    for name in _INS:
        a = _np.ascontiguousarray(inputs[name])
        arrays[f"in_{name}_dram"] = a
        args.append(nc.dram_tensor(f"in_{name}_dram", a.shape, _mybir.dt.from_np(a.dtype), kind="ExternalInput").ap())
    for i, (shape, dtype) in enumerate(_OUTS):
        dt = _mybir.dt.from_np(_np.dtype(dtype))
        args.append(nc.dram_tensor(f"out_{i}_dram", shape, dt, kind="ExternalOutput").ap())
    add_graph_layer(nc, *args)
    r = _run(nc, [arrays], core_ids=[0])
    got = tuple(r.results[0][f"out_{i}_dram"] for i in range(len(_OUTS)))
    return got[0]
```

```python
import concourse.bass as bass
from concourse import mybir
from contextlib import ExitStack

P = 128


def add_graph_layer(nc, x, adj, out):
    fp32 = mybir.dt.float32
    bf16 = mybir.dt.bfloat16
    u32 = mybir.dt.uint32
    u16 = mybir.dt.uint16
    ALU = mybir.AluOpType
    ACT = mybir.ActivationFunctionType
    AX = mybir.AxisListType

    N, D = x.shape
    TILES = N // P
    EPS_NORM = 1e-5
    EPS_HEAD = 1e-12

    SEGS = 8
    SEG = N // SEGS
    CAND = 8 * SEGS
    QUARTERS = 4
    QCOLS = N // QUARTERS
    SEGS_Q = SEGS // QUARTERS
    SLOTS = 24
    BIAS = 128
    TOP = BIAS + N - 1
    OWN = 6
    SPILL = SLOTS - OWN
    EXTRA = 4
    PLACES = EXTRA * P
    PAY = 2 * SPILL + 1
    GROUPS = [(0, 3), (3, OWN)]

    ROWS = 4
    LN = N // (P * ROWS)
    KB = N // P
    HCH = 8
    NCH = KB // HCH

    x_ln = x.rearrange("(c p j) d -> c p j d", p=P, j=ROWS)
    x_t = x.rearrange("(t p) d -> t p d", p=P)
    out_t = out.rearrange("(t p) d -> t p d", p=P)
    adj_t = adj.rearrange("(t p) n -> t p n", p=P)

    ctx = ExitStack()
    with ctx:
        def sb(name, shape, dt):
            return ctx.enter_context(nc.sbuf_tensor(name, shape, dt))

        def sem(name):
            return ctx.enter_context(nc.semaphore(name))

        h = nc.dram_tensor("h_scratch", [N, D], fp32, kind="Internal").ap()
        h_ln = h.rearrange("(c p j) d -> c p j d", p=P, j=ROWS)
        h_blk = h.rearrange("(c k p) d -> c p k d", p=P, k=HCH)

        A = sb("adj_tile", [P, 2, N], fp32)
        G = sb("gathered", [P, 2, OWN + EXTRA, D], fp32)
        diag = sb("diag", [P, 2, OWN, P], fp32)
        ident = sb("ident", [P, P], fp32)
        ones = sb("ones", [P, 1], fp32)
        junk = sb("junk", [P, 2, QCOLS], bf16)
        xres = sb("x_residual", [P, 2, D], fp32)
        osb = sb("out_tile", [P, 2, D], fp32)
        cv = sb("cand_value", [P, 2, CAND], fp32)
        ci = sb("cand_index", [P, 2, CAND], u32)
        segtab = sb("segment_top", [P, SEGS], fp32)
        cif = sb("cand_index_float", [P, CAND], fp32)
        rank0 = sb("rank_all", [P, CAND], fp32)
        rank = sb("rank", [P, CAND], fp32)
        keys = sb("keys", [P, 2, 2, CAND], u32)
        srt = sb("sorted_keys", [P, 2, SLOTS], u32)
        idx = sb("slot_column", [P, 2, SLOTS], u32)
        val = sb("slot_value", [P, 2, SLOTS], u32)
        pos = sb("slot_sign", [P, 2, SLOTS], fp32)
        inc = sb("slot_inc", [P, SLOTS], fp32)
        incn = sb("slot_inc_normed", [P, 2, SLOTS], fp32)
        cnt = sb("count", [P, 2], fp32)
        minus_own = sb("minus_own", [P, 1], fp32)
        sign = sb("cand_sign", [P, 2, CAND], fp32)
        signf = sb("last_sign", [P, 2, SEGS], fp32)
        root = sb("root", [P, 2], fp32)
        rootc = sb("root_clamped", [P, 2], fp32)
        head = sb("head", [P, 1], fp32)
        deg = sb("degree", [P, 1], fp32)
        rdeg = sb("inv_degree", [P, 1], fp32)
        neg_all = sb("negatives", [P, QUARTERS * TILES], fp32)
        full_all = sb("full_segments", [P, TILES], fp32)
        cnt_all = sb("counts", [P, TILES], fp32)
        end_all = sb("spill_end", [P, TILES], fp32)
        negf = sb("negative_flags", [P, QUARTERS * TILES], fp32)
        negs = sb("negative_quarters", [P, TILES], fp32)
        over = sb("overfull", [P, TILES], fp32)
        tri = sb("lanes_before", [P, P], fp32)
        differ = sb("difference", [P, P], bf16)
        placeno = sb("place_number", [P, PLACES], fp32)
        first_of = sb("place_minus_slot", [P, EXTRA, SPILL], fp32)
        spilln = sb("spill_count", [P, 2], fp32)
        pay = sb("spill_payload", [P, 2, PAY], fp32)
        reach = sb("from_first_place", [P, PLACES], bf16)
        owner = sb("owner", [P, PLACES], fp32)
        brought = sb("brought", [P, EXTRA, PAY], fp32)
        hit = sb("own_entry", [P, EXTRA, SPILL], fp32)
        taken = sb("taken", [P, EXTRA, 2, SPILL], fp32)
        sum9 = sb("sum_of_9", [P, EXTRA, 2, SPILL // 2], fp32)
        sum3 = sb("sum_of_3", [P, EXTRA, 2, SPILL // 6], fp32)
        entry = sb("entry", [P, EXTRA, 2], fp32)
        spidx = sb("spill_column", [P, 2, EXTRA], u32)
        W = sb("spill_matrix", [P, 2, EXTRA, P], fp32)
        tnum = sb("tile_number", [1, TILES], fp32)
        badm = sb("bad_rows", [P, TILES], fp32)
        badk = sb("bad_key", [1, TILES], fp32)
        badl = sb("bad_list", [1, TILES], fp32)
        badu = sb("bad_list_int", [1, TILES], u32)
        badn = sb("bad_number", [1, 1], fp32)
        badnu = sb("bad_number_int", [1, 1], u32)
        xin = sb("ln_x", [P, 4, ROWS, D], fp32)
        hst = sb("ln_h", [P, 2, ROWS, D], fp32)
        st = sb("ln_stats", [P, 2, ROWS, 6], fp32)
        mv = sb("ln_mean_var", [P, 2, ROWS, 2], fp32)
        ve = sb("ln_var_eps", [P, 2, ROWS], fp32)
        sd = sb("ln_std", [P, 2, ROWS], fp32)
        rs = sb("ln_rstd", [P, 2, ROWS], fp32)
        nb = sb("ln_bias", [P, 2, ROWS], fp32)
        incT = sb("inc_T", [P, 2, P], fp32)
        dcnt = sb("dense_count", [P, 1], fp32)
        drt = sb("dense_root", [P, 1], fp32)
        drc = sb("dense_root_clamped", [P, 1], fp32)
        dhd = sb("dense_head", [P, 1], fp32)
        ddeg = sb("dense_degree", [P, 1], fp32)
        drd = sb("dense_inv_degree", [P, 1], fp32)

        acc = [ctx.enter_context(nc.psum_tensor(f"acc{b}", [P, D], fp32)) for b in range(2)]
        poff = ctx.enter_context(nc.psum_tensor("poff", [P, 512], fp32))
        powner = ctx.enter_context(nc.psum_tensor("powner", [P, PLACES], fp32))
        pbrought = ctx.enter_context(nc.psum_tensor("pbrought", [P, 512], fp32))
        pturned = ctx.enter_context(nc.psum_tensor("pturned", [P, PLACES], fp32))
        ptr = [ctx.enter_context(nc.psum_tensor(f"ptr{b}", [P, 512], fp32)) for b in range(2)]
        pdense = powner

        const_step = sem("const_step")
        passed = sem("passed")
        consts_set = sem("consts_set")
        zeroed = sem("zeroed")
        ln_loaded = [sem(f"ln_loaded{b}") for b in range(4)]
        ln_stat = sem("ln_stat")
        ln_var = sem("ln_var")
        ln_root = sem("ln_root")
        ln_scaled = sem("ln_scaled")
        ln_done = sem("ln_done")
        h_stored = [sem(f"h_stored{b}") for b in range(4)]
        adj_loaded = [[sem(f"adj_loaded{b}{q}") for q in range(QUARTERS)] for b in range(2)]
        x_loaded = [sem(f"x_loaded{b}") for b in range(2)]
        negs_checked = sem("negs_checked")
        vals_found = sem("vals_found")
        idx_found = sem("idx_found")
        count_ready = sem("count_ready")
        full_ready = sem("full_ready")
        halves_ready = sem("halves_ready")
        rank_step = sem("rank_step")
        ranked = sem("ranked")
        clamped = sem("clamped")
        sign_ready = sem("sign_ready")
        sort = sem("sort")
        unpacked = sem("unpacked")
        spill_counted = sem("spill_counted")
        spill_offset = sem("spill_offset")
        offset_ready = sem("offset_ready")
        pay_ready = sem("pay_ready")
        reach_ready = sem("reach_ready")
        owner_found = sem("owner_found")
        owner_ready = sem("owner_ready")
        spill_brought = sem("spill_brought")
        brought_ready = sem("brought_ready")
        pick = sem("pick")
        spidx_ready = sem("spidx_ready")
        w_ready = sem("w_ready")
        bad_marked = sem("bad_marked")
        bad_summed = sem("bad_summed")
        root_ready = sem("root_ready")
        weigh = sem("weigh")
        inc_ready = sem("inc_ready")
        diag_ready = sem("diag_ready")
        gathered = [[sem(f"gathered{b}{g}") for g in range(len(GROUPS) + 1)] for b in range(2)]
        acc_ready = sem("acc_ready")
        out_ready = sem("out_ready")
        out_stored = [sem(f"out_stored{b}") for b in range(2)]
        list_step = sem("list_step")
        list_ready = sem("list_ready")
        d_adj = sem("d_adj")
        d_x = sem("d_x")
        d_h = [sem(f"d_h{b}") for b in range(2)]
        d_step = sem("d_step")
        d_count = sem("d_count")
        d_root = sem("d_root")
        d_inc = sem("d_inc")
        d_tr = sem("d_tr")
        d_copied = sem("d_copied")
        d_mm = sem("d_mm")
        d_out = sem("d_out")
        d_stored = sem("d_stored")

        def hold(eng, signal, value):
            eng.wait_ge(signal, value)
            eng.sem_inc(passed, 1)

        ROUNDS = SLOTS // 8
        top = [[1 + 4 * r + half for half in range(2)] for r in range(ROUNDS)]
        drop = [[3 + 4 * r + half for half in range(2)] for r in range(ROUNDS - 1)]
        SORT = top[-1][1]

        def sorted_(i, b, n):
            return i * (2 * SORT) + (b * SORT + n)

        block = ctx.enter_context(nc.Block())
        LAST = TILES // 2 - 1

        @block.sync
        def _(sp):
            def ln_load(i, b):
                sp.dma_start(xin[:, b], x_ln[i * 4 + b]).then_inc(ln_loaded[b], 16)

            def ln_store(i, b):
                sp.wait_ge(ln_done, i * 4 + b + 1)
                sp.dma_start(h_ln[i * 4 + b], hst[:, b % 2]).then_inc(h_stored[b], 16)

            def load_tile(i, b):
                for q in range(QUARTERS):
                    hold(sp, idx_found, i * (2 * SEGS) + (b - 2) * SEGS + (q + 1) * SEGS_Q)
                    sp.wait_ge(negs_checked, i * (2 * QUARTERS) + (b - 2) * QUARTERS + q + 1)
                    sp.dma_start(A[:, b, q * QCOLS:(q + 1) * QCOLS],
                                 adj_t[i * 2 + b, :, q * QCOLS:(q + 1) * QCOLS]).then_inc(adj_loaded[b][q], 16)

            def load_x(i, b):
                sp.dma_start(xres[:, b], x_t[i * 2 + b]).then_inc(x_loaded[b], 16)

            def store_tile(i, b):
                hold(sp, out_ready, i * 2 + b + 1)
                sp.dma_start(out_t[i * 2 + b], osb[:, b]).then_inc(out_stored[b], 16)

            for b in range(4):
                ln_load(0, b)
            def ln_chunks(first, end):
                with sp.Fori(first, end) as i:
                    for b in range(4):
                        ln_store(i - 1, b)
                        ln_load(i, b)

            def load_quarter(b, q):
                sp.dma_start(A[:, b, q * QCOLS:(q + 1) * QCOLS],
                             adj_t[b, :, q * QCOLS:(q + 1) * QCOLS]).then_inc(adj_loaded[b][q], 16)

            ln_chunks(1, LN // 8)
            load_quarter(0, 0)
            for c in range(LN // 2, LN):
                ln_store(c // 4 - 1, c % 4)
                ln_load(c // 4, c % 4)
                if c % 2 == 1 and (c - LN // 2) // 2 + 1 < QUARTERS:
                    load_quarter(0, (c - LN // 2) // 2 + 1)
            load_x(0, 0)
            for b in range(4):
                ln_store(LN // 4 - 1, b)
                load_quarter(1, b)
            load_x(0, 1)

            for b in range(2):
                load_tile(1, b)
            with sp.Fori(2, TILES // 2) as i:
                for b in range(2):
                    load_tile(i, b)
                    store_tile(i - 2, b)
                    hold(sp, out_stored[b], i * 16 - 16)
                    load_x(i - 1, b)
            for b in range(2):
                store_tile(LAST - 1, b)
                sp.wait_ge(out_stored[b], 16 * (TILES // 2 - 1))
                load_x(LAST, b)
            for b in range(2):
                store_tile(LAST, b)
            for b in range(2):
                sp.wait_ge(out_stored[b], 16 * (TILES // 2))

            sp.wait_ge(list_ready, 1)
            n = sp.value_load(badnu[0:1, 0:1], min_val=0, max_val=TILES)
            with sp.If(n > 0):
                with sp.Fori(0, n) as j:
                    t = sp.value_load(badu[0:1, bass.ds(j, 1)], min_val=0, max_val=TILES - 1)
                    sp.dma_start(A[:, 0, :], adj_t[t]).then_inc(d_adj, 16)
                    sp.dma_start(xres[:, 0], x_t[t]).then_inc(d_x, 16)
                    for c in range(NCH):
                        if c >= 2:
                            sp.wait_ge(d_mm, j * KB + (c - 1) * HCH)
                        sp.dma_start(G[:, c % 2, 0:HCH, :], h_blk[c]).then_inc(d_h[c % 2], 16)
                    sp.wait_ge(d_out, j + 1)
                    sp.dma_start(out_t[t], osb[:, 0]).then_inc(d_stored, 16)
                    hold(sp, d_stored, j * 16 + 16)

        @block.gpsimd
        def _(pool):
            steps = [0]

            def step(ins):
                steps[0] += 1
                ins.then_inc(const_step, 1)
                pool.wait_ge(const_step, steps[0])

            step(nc.gpsimd.memset(ident[:], 0.0))
            step(nc.gpsimd.affine_select(out=ident[:], in_=ident[:], compare_op=ALU.not_equal, fill=1.0,
                                         base=0, pattern=[[-1, P]], channel_multiplier=1))
            step(nc.gpsimd.memset(ones[:], 1.0))
            step(nc.gpsimd.iota(tnum[:], pattern=[[1, TILES]], base=1, channel_multiplier=0,
                                allow_small_or_imprecise_dtypes=True))
            for s in range(SEGS):
                step(nc.gpsimd.memset(segtab[:, s:s + 1], float(TOP - SEG * s)))
            step(nc.gpsimd.memset(minus_own[:], -float(OWN)))
            step(nc.gpsimd.iota(placeno[:], pattern=[[1, PLACES]], base=0, channel_multiplier=0,
                                allow_small_or_imprecise_dtypes=True))
            step(nc.gpsimd.iota(first_of[:], pattern=[[P, EXTRA], [-1, SPILL]], base=0, channel_multiplier=1,
                                allow_small_or_imprecise_dtypes=True))
            step(nc.gpsimd.memset(differ[:], 0.0))
            step(nc.gpsimd.affine_select(out=differ[:], in_=differ[:], compare_op=ALU.not_equal, fill=1.0,
                                         base=0, pattern=[[-1, P]], channel_multiplier=1))
            step(nc.gpsimd.affine_select(out=differ[:], in_=differ[:], compare_op=ALU.not_equal, fill=-1.0,
                                         base=-1, pattern=[[-1, P]], channel_multiplier=1))
            step(nc.gpsimd.memset(tri[:], 1.0))
            step(nc.gpsimd.affine_select(out=tri[:], in_=tri[:], compare_op=ALU.is_gt, fill=0.0,
                                         base=0, pattern=[[1, P]], channel_multiplier=-1))
            pool.sem_inc(consts_set, 1)
            nc.gpsimd.memset(G[:, 0], 0.0).then_inc(zeroed, 1)
            nc.gpsimd.memset(G[:, 1], 0.0).then_inc(zeroed, 1)

            def gather(b, s, column, done):
                nc.gpsimd.indirect_dma_start(
                    out=G[:, b, s, :], out_offset=None, in_=h[:, :],
                    in_offset=bass.IndirectOffsetOnAxis(ap=column, axis=0),
                    bounds_check=N - 1, oob_is_err=False).then_inc(done, 16)

            PICK = 8

            def mark_reach(i, b, first=False):
                hold(pool, offset_ready, i * 4 + b * 2 + 2)
                if not first:
                    hold(pool, owner_found, i * 2 + b)
                nc.gpsimd.tensor_scalar(reach[:], placeno[:], pay[:, b, PAY - 1:PAY], None,
                                        ALU.is_ge).then_inc(reach_ready, 1)

            def rank_keys(i, b):
                hold(pool, idx_found, i * (2 * SEGS) + (b + 1) * SEGS)
                nc.gpsimd.tensor_copy(cif[:], ci[:, b]).then_inc(rank_step, 1)
                hold(pool, rank_step, i * 6 + b * 3 + 1)
                nc.gpsimd.tensor_tensor(rank0[:].rearrange("p (s e) -> p s e", e=8),
                                        segtab[:].unsqueeze(2).broadcast_to([P, SEGS, 8]),
                                        cif[:].rearrange("p (s e) -> p s e", e=8), ALU.subtract).then_inc(rank_step, 1)
                hold(pool, rank_step, i * 6 + b * 3 + 2)
                hold(pool, full_ready, i * 4 + b * 2 + 2)
                k16 = keys[:, b].bitcast(u16).rearrange("p l (c h) -> p l c h", h=2)
                nc.gpsimd.tensor_tensor(rank[:], sign[:, b], rank0[:], ALU.mult).then_inc(rank_step, 1)
                hold(pool, rank_step, i * 6 + b * 3 + 3)
                nc.gpsimd.tensor_copy(k16[:, :, :, 1],
                                      rank[:].unsqueeze(1).broadcast_to([P, 2, CAND])).then_inc(ranked, 1)
                nc.gpsimd.tensor_scalar(rootc[:, b:b + 1], root[:, b:b + 1], EPS_HEAD, None,
                                        ALU.max).then_inc(clamped, 1)

            def gather_tile(i, b, after, first=False):
                if not first:
                    hold(pool, acc_ready, i * 2 + b - 1)
                hold(pool, unpacked, i * 6 + b * 3 + 3)
                for s in range(OWN):
                    gather(b, s, idx[:, b, s:s + 1], gathered[b][0 if s < GROUPS[0][1] else 1])

                if after:
                    mark_reach(*after)
                    rank_keys(*after)

                n = [0]

                def next_step(ins):
                    n[0] += 1
                    ins.then_inc(pick, 1)
                    hold(pool, pick, i * (2 * PICK) + (b * PICK + n[0]))

                hold(pool, brought_ready, i * 2 + b + 1)
                next_step(nc.gpsimd.tensor_tensor(
                    hit[:], brought[:, :, PAY - 1:PAY].broadcast_to([P, EXTRA, SPILL]), first_of[:], ALU.subtract))
                next_step(nc.gpsimd.tensor_scalar(hit[:], hit[:], 0.0, None, ALU.is_equal))
                next_step(nc.gpsimd.tensor_tensor(
                    taken[:], brought[:, :, 0:2 * SPILL].rearrange("p g (c k) -> p g c k", c=2),
                    hit[:].unsqueeze(2).broadcast_to([P, EXTRA, 2, SPILL]), ALU.mult))
                next_step(nc.gpsimd.tensor_tensor(sum9[:], taken[:, :, :, 0:SPILL // 2],
                                                  taken[:, :, :, SPILL // 2:], ALU.add))
                third = SPILL // 6
                next_step(nc.gpsimd.tensor_tensor(sum3[:], sum9[:, :, :, 0:third], sum9[:, :, :, third:2 * third],
                                                  ALU.add))
                next_step(nc.gpsimd.tensor_tensor(sum3[:], sum3[:], sum9[:, :, :, 2 * third:], ALU.add))
                next_step(nc.gpsimd.tensor_tensor(entry[:].unsqueeze(3), sum3[:, :, :, 0:1], sum3[:, :, :, 1:2], ALU.add))
                next_step(nc.gpsimd.tensor_tensor(entry[:].unsqueeze(3), entry[:].unsqueeze(3), sum3[:, :, :, 2:3], ALU.add))
                nc.gpsimd.tensor_scalar(spidx[:, b], entry[:, :, 0], -1.0, float(TOP), ALU.mult,
                                        ALU.add).then_inc(spidx_ready, 1)
                hold(pool, spidx_ready, i * 2 + b + 1)
                for g in range(EXTRA):
                    gather(b, OWN + g, spidx[:, b, g:g + 1], gathered[b][2])

            mark_reach(0, 0, first=True)
            rank_keys(0, 0)
            pool.wait_ge(zeroed, 2)
            for b in range(4):
                pool.wait_ge(h_stored[b], 16 * (LN // 4))
            gather_tile(0, 0, (0, 1), first=True)
            gather_tile(0, 1, (1, 0), first=True)
            with pool.Fori(1, LAST) as i:
                gather_tile(i, 0, (i, 1))
                gather_tile(i, 1, (i + 1, 0))
            gather_tile(LAST, 0, (LAST, 1))
            gather_tile(LAST, 1, None)

        @block.scalar
        def _(act):
            def ln_sqrt(i, b):
                act.wait_ge(ln_var, i * 4 + b + 1)
                nc.scalar.activation(sd[:, b % 2], ve[:, b % 2], ACT.Sqrt).then_inc(ln_root, 1)

            def ln_apply(i, b, first=False):
                act.wait_ge(ln_scaled, i * 4 + b + 1)
                if not first or b >= 2:
                    act.wait_ge(h_stored[(b + 2) % 4], i * 16 + 16 * (b >= 2))
                for j in range(ROWS):
                    last = nc.scalar.activation(hst[:, b % 2, j], xin[:, b, j], ACT.Relu,
                                                bias=nb[:, b % 2, j:j + 1], scale=rs[:, b % 2, j:j + 1])
                last.then_inc(ln_done, 1)

            for b in range(4):
                ln_sqrt(0, b)
                ln_apply(0, b, first=True)

            act.wait_ge(consts_set, 1)

            def check(i, b, q, first=False):
                if not first:
                    act.wait_ge(negs_checked, i * (2 * QUARTERS) + b * QUARTERS + q - 1)
                act.wait_ge(adj_loaded[b][q], i * 16 + 16)
                nc.scalar.activation(junk[:, q % 2], A[:, b, q * QCOLS:(q + 1) * QCOLS], ACT.Relu, scale=-1.0,
                                     accum_out=neg_all[:, bass.ds(i * (2 * QUARTERS) + (b * QUARTERS + q), 1)]
                                     ).then_inc(negs_checked, 1)

            def keys16(b, half):
                return keys[:, b, half].bitcast(u16).rearrange("p (c h) -> p c h", h=2)

            cv16 = [cv[:, b].bitcast(u16).rearrange("p (c h) -> p c h", h=2) for b in range(2)]

            def heads(i, b, first=False):
                act.wait_ge(vals_found, i * (2 * SEGS) + (b + 1) * SEGS)
                if not first:
                    act.wait_ge(full_ready, i * 4 + b * 2 - 2)
                nc.scalar.activation(sign[:, b], cv[:, b], ACT.Sign,
                                     accum_out=cnt[:, b:b + 1]).then_inc(count_ready, 1)
                for half in range(2):
                    nc.scalar.activation(keys16(b, half)[:, :, 0], cv16[b][:, :, 1 - half],
                                         ACT.Copy).then_inc(halves_ready, 1)
                act.wait_ge(count_ready, i * 2 + b + 1)
                nc.scalar.activation(spilln[:, b:b + 1], cnt[:, b:b + 1], ACT.Relu,
                                     bias=minus_own[:]).then_inc(spill_counted, 1)
                nc.scalar.activation(root[:, b:b + 1], cnt[:, b:b + 1], ACT.Sqrt).then_inc(root_ready, 1)
                nc.scalar.activation(signf[:, b], cv[:, b, 7::8], ACT.Sign,
                                     accum_out=full_all[:, bass.ds(i * 2 + b, 1)]).then_inc(full_ready, 1)
                nc.scalar.activation(cnt_all[:, bass.ds(i * 2 + b, 1)], cnt[:, b:b + 1],
                                     ACT.Copy).then_inc(full_ready, 1)

            def unpack(i, b):
                act.wait_ge(sort, sorted_(i, b, SORT))
                v16 = val[:, b].bitcast(u16).rearrange("p (s h) -> p s h", h=2)
                s16 = [srt[:, half].bitcast(u16).rearrange("p (s h) -> p s h", h=2) for half in range(2)]
                nc.scalar.activation(pay[:, b, 0:SPILL], s16[0][:, OWN:, 1], ACT.Copy).then_inc(pay_ready, 1)
                nc.scalar.activation(idx[:, b], s16[0][:, :, 1], ACT.Copy, bias=float(TOP),
                                     scale=-1.0).then_inc(unpacked, 1)
                nc.scalar.activation(v16[:, :, 1], s16[0][:, :, 0], ACT.Copy).then_inc(unpacked, 1)
                nc.scalar.activation(v16[:, :, 0], s16[1][:, :, 0], ACT.Copy).then_inc(unpacked, 1)

            def first_places(i, b):
                act.wait_ge(spill_offset, i * 2 + b + 1)
                nc.scalar.activation(pay[:, b, PAY - 1:PAY], poff[:, 0:1], ACT.Copy).then_inc(offset_ready, 1)
                nc.scalar.activation(end_all[:, bass.ds(i * 2 + b, 1)], poff[:, 0:1], ACT.Identity,
                                     bias=spilln[:, b:b + 1]).then_inc(offset_ready, 1)

            def copy_owner(i, b):
                act.wait_ge(owner_found, i * 2 + b + 1)
                nc.scalar.activation(owner[:], powner[:], ACT.Copy).then_inc(owner_ready, 1)

            def slot_signs(i, b):
                act.wait_ge(unpacked, i * 6 + b * 3 + 3)
                nc.scalar.activation(pos[:, b], val[:, b].bitcast(fp32), ACT.Sign).then_inc(sign_ready, 1)

            def diag_tile(i, b):
                act.wait_ge(inc_ready, i * 2 + b + 1)
                nc.scalar.activation(pay[:, b, SPILL:2 * SPILL], incn[:, b, OWN:], ACT.Copy).then_inc(pay_ready, 1)
                for lo, hi in GROUPS:
                    for s in range(lo, hi):
                        last = nc.scalar.activation(diag[:, b, s], ident[:], ACT.Copy, scale=incn[:, b, s:s + 1])
                    last.then_inc(diag_ready, 1)

            def copy_brought(i, b):
                act.wait_ge(spill_brought, i * 2 + b + 1)
                nc.scalar.activation(brought[:], pbrought[:, 0:EXTRA * PAY].rearrange("p (g c) -> p g c", g=EXTRA),
                                     ACT.Copy).then_inc(brought_ready, 1)

            def spill_matrix(i, b):
                act.wait_ge(spidx_ready, i * 2 + b + 1)
                for g in range(EXTRA):
                    last = nc.scalar.activation(W[:, b, g], pturned[:, g * P:(g + 1) * P], ACT.Copy,
                                                scale=entry[:, g, 1:2])
                last.then_inc(w_ready, 1)

            def finish_tile(i, b):
                act.wait_ge(acc_ready, i * 2 + b + 1)
                nc.scalar.activation(osb[:, b], acc[b][:], ACT.Copy).then_inc(out_ready, 1)

            def period(t, t1, t2, after, first=False):
                unpack(*t1)
                heads(*t, first=first)
                slot_signs(*t1)
                first_places(*t)
                for q in range(QUARTERS // 2):
                    if after:
                        check(*after, q)
                if t2:
                    finish_tile(*t2)
                diag_tile(*t1)
                copy_brought(*t1)
                copy_owner(*t)
                for q in range(QUARTERS // 2, QUARTERS):
                    if after:
                        check(*after, q)
                spill_matrix(*t1)

            with act.Fori(1, LN // 8) as i:
                for b in range(4):
                    ln_sqrt(i, b)
                    ln_apply(i, b)
            for c in range(LN // 2, LN):
                ln_sqrt(c // 4, c % 4)
                ln_apply(c // 4, c % 4)
                if c % 2 == 1:
                    q = (c - LN // 2) // 2
                    check(0, 0, q, first=q < 2)
            heads(0, 0, first=True)
            first_places(0, 0)
            copy_owner(0, 0)
            for q in range(QUARTERS):
                check(0, 1, q)
            period((0, 1), (0, 0), None, (1, 0), first=True)
            period((1, 0), (0, 1), (0, 0), (1, 1))
            with act.Fori(1, LAST) as i:
                period((i, 1), (i, 0), (i - 1, 1), (i + 1, 0))
                period((i + 1, 0), (i, 1), (i, 0), (i + 1, 1))
            unpack(LAST, 0)
            heads(LAST, 1)
            slot_signs(LAST, 0)
            first_places(LAST, 1)
            finish_tile(LAST - 1, 1)
            diag_tile(LAST, 0)
            copy_brought(LAST, 0)
            copy_owner(LAST, 1)
            unpack(LAST, 1)
            slot_signs(LAST, 1)
            spill_matrix(LAST, 0)
            diag_tile(LAST, 1)
            copy_brought(LAST, 1)
            finish_tile(LAST, 0)
            spill_matrix(LAST, 1)
            finish_tile(LAST, 1)

            act.wait_ge(list_ready, 1)
            n = act.value_load(badnu[0:1, 0:1], min_val=0, max_val=TILES)
            with act.If(n > 0):
                with act.Fori(0, n) as j:
                    act.wait_ge(d_count, j + 1)
                    nc.scalar.activation(drt[:], dcnt[:], ACT.Sqrt).then_inc(d_root, 1)

        @block.vector
        def _(dve):
            LNS = ROWS + ROWS + 1

            def ln_chunk(i, b):
                base = i * (4 * LNS) + b * LNS
                p = b % 2
                dve.wait_ge(ln_loaded[b], i * 16 + 16)
                for j in range(ROWS):
                    nc.vector.bn_stats(st[:, p, j], xin[:, b, j]).then_inc(ln_stat, 1)
                for j in range(ROWS):
                    hold(dve, ln_stat, base + j + 1)
                    nc.vector.bn_aggr(mv[:, p, j], st[:, p, j]).then_inc(ln_stat, 1)
                dve.wait_ge(ln_stat, base + 2 * ROWS)
                nc.vector.tensor_scalar(ve[:, p], mv[:, p, :, 1], EPS_NORM, None, ALU.add).then_inc(ln_var, 1)
                dve.wait_ge(ln_root, i * 4 + b + 1)
                nc.vector.reciprocal(rs[:, p], sd[:, p]).then_inc(ln_stat, 1)
                dve.wait_ge(ln_stat, base + LNS)
                nc.vector.scalar_tensor_tensor(out=nb[:, p], in0=mv[:, p, :, 0], scalar=-1.0, in1=rs[:, p],
                                               op0=ALU.mult, op1=ALU.mult).then_inc(ln_scaled, 1)

            for b in range(2):
                ln_chunk(0, b)
            for b in range(2, 4):
                dve.wait_ge(ln_done, b - 1)
                ln_chunk(0, b)

            dve.wait_ge(consts_set, 1)

            def find_values(i, b, g):
                if g % SEGS_Q == 0:
                    hold(dve, adj_loaded[b][g // SEGS_Q], i * 16 + 16)
                nc.vector.max(out=cv[:, b, 8 * g:8 * g + 8],
                              in_=A[:, b, g * SEG:(g + 1) * SEG]).then_inc(vals_found, 1)

            def find_places(i, b, g):
                hold(dve, vals_found, i * (2 * SEGS) + b * SEGS + g + 1)
                nc.vector.max_index(out=ci[:, b, 8 * g:8 * g + 8], in_max=cv[:, b, 8 * g:8 * g + 8],
                                    in_values=A[:, b, g * SEG:(g + 1) * SEG]).then_inc(idx_found, 1)

            def take_top(i, b, r):
                if r == 0:
                    hold(dve, ranked, i * 2 + b + 1)
                    hold(dve, halves_ready, i * 4 + b * 2 + 2)
                for half in range(2):
                    if r:
                        hold(dve, sort, sorted_(i, b, drop[r - 1][half]))
                    nc.vector.max(out=srt[:, half, 8 * r:8 * r + 8].bitcast(fp32),
                                  in_=keys[:, b, half].bitcast(fp32)).then_inc(sort, 1)

            def drop_top(i, b, r):
                for half in range(2):
                    k = keys[:, b, half].bitcast(fp32)
                    hold(dve, sort, sorted_(i, b, top[r][half]))
                    nc.vector.match_replace(out=k, in_to_replace=srt[:, half, 8 * r:8 * r + 8].bitcast(fp32),
                                            in_values=k, imm_value=0.0).then_inc(sort, 1)

            WEIGH = 3

            def weigh_1(i, b):
                dve.wait_ge(clamped, i * 2 + b + 1)
                nc.vector.reciprocal(head[:], rootc[:, b:b + 1]).then_inc(weigh, 1)

            def weigh_2(i, b):
                dve.wait_ge(sign_ready, i * 2 + b + 1)
                dve.wait_ge(weigh, i * (2 * WEIGH) + (b * WEIGH + 1))
                nc.vector.scalar_tensor_tensor(out=inc[:], in0=pos[:, b], scalar=head[:], in1=val[:, b].bitcast(fp32),
                                               op0=ALU.mult, op1=ALU.add, accum_out=deg[:]).then_inc(weigh, 1)

            def weigh_3(i, b):
                dve.wait_ge(weigh, i * (2 * WEIGH) + (b * WEIGH + 2))
                nc.vector.reciprocal(rdeg[:], deg[:]).then_inc(weigh, 1)

            def weigh_4(i, b):
                dve.wait_ge(weigh, i * (2 * WEIGH) + (b * WEIGH + 3))
                nc.vector.tensor_scalar(incn[:, b], inc[:], rdeg[:], None, ALU.mult).then_inc(inc_ready, 1)

            def period(t, t1):
                for g in range(SEGS):
                    if t:
                        find_values(*t, g)
                    if t1:
                        if g >= 2 and g < 7 and g % 2 == 0:
                            take_top(*t1, (g - 2) // 2)
                        if g >= 2 and g < 6 and g % 2 == 1:
                            drop_top(*t1, (g - 2) // 2)
                for g in range(SEGS):
                    if t:
                        find_places(*t, g)
                    if t1:
                        if g == 1:
                            weigh_1(*t1)
                        if g == 2:
                            weigh_2(*t1)
                        if g == 3:
                            weigh_3(*t1)
                        if g == 4:
                            weigh_4(*t1)

            with dve.Fori(1, LN // 8) as i:
                for b in range(4):
                    dve.wait_ge(ln_done, i * 4 + b - 1)
                    ln_chunk(i, b)
            for c in range(LN // 2, LN):
                dve.wait_ge(ln_done, c - 1)
                ln_chunk(c // 4, c % 4)
                find_values(0, 0, c - LN // 2)
                if c > LN // 2:
                    find_places(0, 0, c - LN // 2 - 1)
            find_places(0, 0, SEGS - 1)
            period((0, 1), (0, 0))
            with dve.Fori(1, TILES // 2) as i:
                period((i, 0), (i - 1, 1))
                period((i, 1), (i, 0))
            period(None, (LAST, 1))

            steps = [0]

            def step(ins):
                steps[0] += 1
                ins.then_inc(list_step, 1)
                dve.wait_ge(list_step, steps[0])

            dve.wait_ge(negs_checked, TILES * QUARTERS)
            step(nc.vector.tensor_scalar(negf[:], neg_all[:], 0.0, None, ALU.not_equal))
            step(nc.vector.tensor_reduce(negs[:], negf[:].rearrange("p (t q) -> p t q", q=QUARTERS),
                                         axis=AX.X, op=ALU.add))
            dve.wait_ge(full_ready, TILES * 2)
            step(nc.vector.scalar_tensor_tensor(out=over[:], in0=cnt_all[:], scalar=float(SLOTS), in1=full_all[:],
                                                op0=ALU.is_gt, op1=ALU.add))
            step(nc.vector.tensor_tensor(over[:], over[:], negs[:], ALU.add))
            step(nc.vector.scalar_tensor_tensor(out=over[:], in0=cnt_all[:], scalar=0.5, in1=over[:],
                                                op0=ALU.is_lt, op1=ALU.add))
            dve.wait_ge(offset_ready, TILES * 2)
            nc.vector.scalar_tensor_tensor(out=badm[:], in0=end_all[:], scalar=float(PLACES), in1=over[:],
                                           op0=ALU.is_gt, op1=ALU.add).then_inc(bad_marked, 1)
            dve.wait_ge(bad_summed, 1)
            step(nc.vector.tensor_scalar(badk[:], poff[0:1, 0:TILES], 0.0, 0.0, ALU.is_gt, ALU.add,
                                         accum_out=badn[:]))
            step(nc.vector.tensor_copy(badnu[:], badn[:]))
            step(nc.vector.tensor_tensor(badk[:], badk[:], tnum[:], ALU.mult))
            for r in range(TILES // 8):
                e = slice(8 * r, 8 * r + 8)
                step(nc.vector.max(out=badl[:, e], in_=badk[:]))
                step(nc.vector.match_replace(out=badk[:], in_to_replace=badl[:, e], in_values=badk[:],
                                             imm_value=0.0))
            nc.vector.tensor_scalar(badu[:], badl[:], -1.0, 0.0, ALU.add, ALU.max).then_inc(list_ready, 1)

            dve.wait_ge(list_ready, 1)
            n = dve.value_load(badnu[0:1, 0:1], min_val=0, max_val=TILES)
            D_STEPS = 3
            with dve.If(n > 0):
                with dve.Fori(0, n) as j:
                    dve.wait_ge(d_adj, j * 16 + 16)
                    nc.vector.tensor_scalar(A[:, 1, :], A[:, 0, :], 0.0, 0.0, ALU.is_gt, ALU.add,
                                            accum_out=dcnt[:]).then_inc(d_count, 1)
                    dve.wait_ge(d_root, j + 1)
                    nc.vector.tensor_scalar(drc[:], drt[:], EPS_HEAD, None, ALU.max).then_inc(d_step, 1)
                    dve.wait_ge(d_step, j * D_STEPS + 1)
                    nc.vector.reciprocal(dhd[:], drc[:]).then_inc(d_step, 1)
                    dve.wait_ge(d_step, j * D_STEPS + 2)
                    nc.vector.scalar_tensor_tensor(out=A[:, 0, :], in0=A[:, 1, :], scalar=dhd[:], in1=A[:, 0, :],
                                                   op0=ALU.mult, op1=ALU.add, accum_out=ddeg[:]).then_inc(d_inc, 1)
                    dve.wait_ge(d_inc, j + 1)
                    nc.vector.reciprocal(drd[:], ddeg[:]).then_inc(d_step, 1)
                    for k in range(KB):
                        dve.wait_ge(d_tr, j * KB + k + 1)
                        if k >= 2:
                            dve.wait_ge(d_mm, j * KB + k - 1)
                        nc.vector.tensor_copy(incT[:, k % 2], ptr[k % 2][:, 0:P]).then_inc(d_copied, 1)
                    dve.wait_ge(d_mm, j * KB + KB)
                    dve.wait_ge(d_step, j * D_STEPS + D_STEPS)
                    dve.wait_ge(d_x, j * 16 + 16)
                    nc.vector.scalar_tensor_tensor(out=osb[:, 0], in0=pdense[:], scalar=drd[:], in1=xres[:, 0],
                                                   op0=ALU.mult, op1=ALU.add).then_inc(d_out, 1)

        @block.tensor
        def _(pe):
            pe.wait_ge(consts_set, 1)

            def offsets(i, b):
                pe.wait_ge(spill_counted, i * 2 + b + 1)
                nc.tensor.matmul(poff[:, 0:1], tri[:], spilln[:, b:b + 1], start=True, stop=True).then_inc(spill_offset, 1)

            def find_owner(i, b, first=False):
                if not first:
                    pe.wait_ge(owner_ready, i * 2 + b)
                pe.wait_ge(reach_ready, i * 2 + b + 1)
                nc.tensor.matmul(powner[:], differ[:], reach[:], start=True, stop=True).then_inc(owner_found, 1)

            def bring_spill(i, b):
                pe.wait_ge(owner_ready, i * 2 + b + 1)
                pe.wait_ge(pay_ready, i * 4 + b * 2 + 2)
                for g in range(EXTRA):
                    of_group = owner[:, g * P:(g + 1) * P]
                    nc.tensor.matmul(pbrought[:, g * PAY:(g + 1) * PAY], of_group, pay[:, b], start=True, stop=True)
                    last = nc.tensor.matmul(pturned[:, g * P:(g + 1) * P], of_group, ident[:], start=True, stop=True)
                last.then_inc(spill_brought, 1)

            def product_own(i, b, first=False):
                if not first:
                    pe.wait_ge(out_ready, i * 2 + b - 1)
                pe.wait_ge(x_loaded[b], i * 16 + 16)
                nc.tensor.matmul(acc[b][:], ident[:], xres[:, b], start=True, stop=False)
                for g, (lo, hi) in enumerate(GROUPS):
                    pe.wait_ge(diag_ready, i * (2 * len(GROUPS)) + b * len(GROUPS) + g + 1)
                    pe.wait_ge(gathered[b][g], i * (16 * (hi - lo)) + 16 * (hi - lo))
                    for s in range(lo, hi):
                        nc.tensor.matmul(acc[b][:], diag[:, b, s], G[:, b, s], start=False, stop=False)

            def product_spill(i, b):
                pe.wait_ge(w_ready, i * 2 + b + 1)
                pe.wait_ge(gathered[b][len(GROUPS)], i * (16 * EXTRA) + 16 * EXTRA)
                for g in range(EXTRA):
                    last = nc.tensor.matmul(acc[b][:], W[:, b, g], G[:, b, OWN + g], start=False,
                                            stop=(g == EXTRA - 1))
                last.then_inc(acc_ready, 1)

            def period(t, t1, t2, first=False):
                if t:
                    offsets(*t)
                if t2:
                    product_spill(*t2)
                bring_spill(*t1)
                if t:
                    find_owner(*t)
                product_own(*t1, first=first)

            offsets(0, 0)
            find_owner(0, 0, first=True)
            period((0, 1), (0, 0), None, first=True)
            period((1, 0), (0, 1), (0, 0), first=True)
            with pe.Fori(1, LAST) as i:
                period((i, 1), (i, 0), (i - 1, 1))
                period((i + 1, 0), (i, 1), (i, 0))
            period((LAST, 1), (LAST, 0), (LAST - 1, 1))
            bring_spill(LAST, 1)
            product_spill(LAST, 0)
            product_own(LAST, 1)
            pe.wait_ge(bad_marked, 1)
            nc.tensor.matmul(poff[0:1, 0:TILES], ones[:], badm[:], start=True, stop=True).then_inc(bad_summed, 1)
            product_spill(LAST, 1)

            pe.wait_ge(list_ready, 1)
            n = pe.value_load(badnu[0:1, 0:1], min_val=0, max_val=TILES)
            with pe.If(n > 0):
                with pe.Fori(0, n) as j:
                    pe.wait_ge(d_inc, j + 1)
                    for k in range(KB + 1):
                        if k < KB:
                            if k >= 2:
                                pe.wait_ge(d_copied, j * KB + k - 1)
                            nc.tensor.transpose(ptr[k % 2][:, 0:P], A[:, 0, k * P:(k + 1) * P],
                                                ident[:]).then_inc(d_tr, 1)
                        if k >= 1:
                            m = k - 1
                            pe.wait_ge(d_copied, j * KB + m + 1)
                            if m % HCH == 0:
                                pe.wait_ge(d_h[m // HCH % 2], j * (16 * NCH // 2) + 16 * (m // HCH // 2 + 1))
                            nc.tensor.matmul(pdense[:], incT[:, m % 2], G[:, m // HCH % 2, m % HCH],
                                             start=(m == 0), stop=(m == KB - 1)).then_inc(d_mm, 1)


_INS = ['x', 'adj']
_OUTS = [((8192, 512), 'float32')]


def kernel(**inputs):
    import numpy as _np
    import concourse.bacc as _bacc
    from concourse import mybir as _mybir
    from concourse.bass_utils import run_bass_kernel_spmd as _run

    nc = _bacc.Bacc("TRN2", target_bir_lowering=False, num_devices=1)
    arrays, args = {}, []
    for name in _INS:
        a = _np.ascontiguousarray(inputs[name])
        arrays[f"in_{name}_dram"] = a
        args.append(nc.dram_tensor(f"in_{name}_dram", a.shape, _mybir.dt.from_np(a.dtype), kind="ExternalInput").ap())
    for i, (shape, dtype) in enumerate(_OUTS):
        dt = _mybir.dt.from_np(_np.dtype(dtype))
        args.append(nc.dram_tensor(f"out_{i}_dram", shape, dt, kind="ExternalOutput").ap())
    add_graph_layer(nc, *args)
    r = _run(nc, [arrays], core_ids=[0])
    got = tuple(r.results[0][f"out_{i}_dram"] for i in range(len(_OUTS)))
    return got[0]
```
